# Optimizing a Trainium2 kernel written in Bass

```python
import numpy as np
import jax
import jax.numpy as jnp

def _softmax(x, axis=-1):
    return jax.nn.softmax(x, axis=axis)

def _gelu(x):
    return jax.nn.gelu(x, approximate=True)

def _silu(x):
    return jax.nn.silu(x)

def _sigmoid(x):
    return jax.nn.sigmoid(x)

def _layernorm(x, axis=-1, eps=1e-05):
    m = jnp.mean(x, axis=axis, keepdims=True)
    v = jnp.var(x, axis=axis, keepdims=True)
    return (x - m) / jnp.sqrt(v + eps)

def _scatter_add(tgt, idx, src, axis=0):
    return tgt.at[idx].add(src)

def _segment_sum(src, seg, n):
    return jax.ops.segment_sum(src, seg, n)
kernel_name = 'mk_gnn_preln_d4_gnn_r32_1c4498'

def setup_inputs(seed: int=0):
    np.random.seed(seed)
    _w = jnp.asarray

    def _rec_inputs():
        import jax
        import jax.numpy as jnp
        _gk = jax.random.key(seed)
        x = -0.0003713 + 1 * jax.random.normal(jax.random.fold_in(_gk, 1), (3125, 256), jnp.float32)
        _s = jax.random.randint(jax.random.fold_in(_gk, 2), (25000,), 0, 3125, jnp.int32)
        _d = jax.random.randint(jax.random.fold_in(_gk, 3), (25000,), 0, 3125, jnp.int32)
        _loop = jnp.arange(3125, dtype=jnp.int32)
        src = jnp.concatenate([_s, _d, _loop])
        dst = jnp.concatenate([_d, _s, _loop])
        _o = jnp.argsort(dst, stable=True)
        src = src[_o]
        dst = dst[_o]
        edge_type_64 = jax.random.randint(jax.random.fold_in(_gk, 12), (53125,), 0, 64, jnp.int32)
        edge_weight = jax.random.uniform(jax.random.fold_in(_gk, 13), (53125,), jnp.float32, 0.0, 0.999998)
        return (x, src, dst, edge_type_64, edge_weight)
    x, src, dst, edge_type_64, edge_weight = _rec_inputs()

    def _L0_gnn_setup():
        import jax, jax.numpy as jnp
        import numpy as np
        N, IN_CH, HEADS, OUT_CH, E = (50000, 256, 4, 64, 25000)
        key = jax.random.key(seed)
        k1, k2, k3, k4, k5 = jax.random.split(key, 5)
        x = jax.random.normal(k1, (N, IN_CH), dtype=jnp.float32)
        edge_index = jax.random.randint(k2, (2, E), 0, N, dtype=jnp.int64)
        bw = float(np.sqrt(6.0 / (IN_CH + HEADS * OUT_CH)))
        ba = float(np.sqrt(6.0 / (HEADS + OUT_CH)))
        weight = jax.random.uniform(k3, (IN_CH, HEADS * OUT_CH), jnp.float32, -bw, bw)
        attn_l = jax.random.uniform(k4, (HEADS, OUT_CH), jnp.float32, -ba, ba)
        attn_r = jax.random.uniform(k5, (HEADS, OUT_CH), jnp.float32, -ba, ba)
        return {'x': x, 'edge_index': edge_index, 'weight': weight, 'attn_l': attn_l, 'attn_r': attn_r}
    _L0_gnn_all = _L0_gnn_setup()
    _L0_gnn_in = {k: v for k, v in _L0_gnn_all.items() if k in ('weight', 'attn_l', 'attn_r')}
    del _L0_gnn_all

    def _L1_gnn_setup():
        import jax, jax.numpy as jnp
        import numpy as np
        N, E, D_IN, D_OUT = (50000, 50000, 256, 256)
        key = jax.random.key(seed)
        k1, k2, k3, k4, k5, k6 = jax.random.split(key, 6)
        x = jax.random.normal(k1, (N, D_IN), dtype=jnp.float32)
        edge_index = jax.random.randint(k2, (2, E), 0, N, dtype=jnp.int64)
        s = 1.0 / np.sqrt(D_IN)
        W1 = jax.random.uniform(k3, (D_OUT, D_IN), minval=-s, maxval=s, dtype=jnp.float32)
        b1 = jax.random.uniform(k4, (D_OUT,), minval=-s, maxval=s, dtype=jnp.float32)
        W2 = jax.random.uniform(k5, (D_OUT, D_IN), minval=-s, maxval=s, dtype=jnp.float32)
        b2 = jax.random.uniform(k6, (D_OUT,), minval=-s, maxval=s, dtype=jnp.float32)
        return {'x': x, 'W1': W1, 'b1': b1, 'W2': W2, 'b2': b2, 'edge_index': edge_index}
    _L1_gnn_all = _L1_gnn_setup()
    _L1_gnn_in = {k: v for k, v in _L1_gnn_all.items() if k in ('W1', 'b1', 'W2', 'b2')}
    del _L1_gnn_all

    def _L2_gnn_setup():
        import jax, jax.numpy as jnp
        import numpy as np
        N_NODES = 50000
        N_EDGES = 15625
        IN_DIM = 256
        HID = 64
        HEADS = 4
        N_REL = 64
        key = jax.random.key(seed)
        ks = jax.random.split(key, 16)
        s = 0.02
        return {'node_features': jax.random.normal(ks[0], (N_NODES, IN_DIM), jnp.float32), 'edge_index': jax.random.randint(ks[1], (2, N_EDGES), 0, N_NODES, jnp.int32), 'edge_relations': jax.random.randint(ks[2], (N_EDGES,), 0, N_REL, jnp.int32), 'query_emb': jax.random.normal(ks[3], (IN_DIM,), jnp.float32), 'Wq': jax.random.normal(ks[4], (IN_DIM, HID * HEADS), jnp.float32) * s, 'bq': jnp.zeros((HID * HEADS,), jnp.float32), 'Wk': jax.random.normal(ks[5], (IN_DIM, HID * HEADS), jnp.float32) * s, 'bk': jnp.zeros((HID * HEADS,), jnp.float32), 'Wv': jax.random.normal(ks[6], (IN_DIM, HID * HEADS), jnp.float32) * s, 'bv': jnp.zeros((HID * HEADS,), jnp.float32), 'rel_w': jax.random.normal(ks[7], (N_REL, HID), jnp.float32) * s, 'Wo': jax.random.normal(ks[8], (HID * HEADS, IN_DIM), jnp.float32) * s, 'bo': jnp.zeros((IN_DIM,), jnp.float32), 'gamma': jnp.ones((IN_DIM,), jnp.float32), 'beta': jnp.zeros((IN_DIM,), jnp.float32)}
    _L2_gnn_all = _L2_gnn_setup()
    _L2_gnn_in = {k: v for k, v in _L2_gnn_all.items() if k in ('query_emb', 'Wq', 'bq', 'Wk', 'bk', 'Wv', 'bv', 'rel_w', 'Wo', 'bo', 'gamma', 'beta')}
    del _L2_gnn_all

    def _L3_gnn_setup():
        import jax, jax.numpy as jnp
        import numpy as np
        N_NODES = 50000
        N_EDGES = 25000
        IN_DIM, HID_DIM, OUT_DIM, N_HEADS = (256, 256, 64, 4)
        ATT_DIM = OUT_DIM * 2 + 1
        key = jax.random.key(seed)
        ks = jax.random.split(key, 8)
        s = 0.05
        return {'x': jax.random.normal(ks[0], (N_NODES, IN_DIM), dtype=jnp.float32), 'idx': jax.random.randint(ks[1], (2, N_EDGES), 0, N_NODES, dtype=jnp.int32), 'elem': jax.random.uniform(ks[2], (N_EDGES,), dtype=jnp.float32), 'W1': jax.random.normal(ks[3], (N_HEADS, IN_DIM, HID_DIM), dtype=jnp.float32) * s, 'b1': jnp.zeros((N_HEADS, HID_DIM), jnp.float32), 'W2': jax.random.normal(ks[4], (N_HEADS, HID_DIM, OUT_DIM), dtype=jnp.float32) * s, 'b2': jnp.zeros((N_HEADS, OUT_DIM), jnp.float32), 'A1': jax.random.normal(ks[5], (N_HEADS, ATT_DIM, ATT_DIM), dtype=jnp.float32) * s, 'ab1': jnp.zeros((N_HEADS, ATT_DIM), jnp.float32), 'A2': jax.random.normal(ks[6], (N_HEADS, ATT_DIM, 1), dtype=jnp.float32) * s, 'ab2': jnp.zeros((N_HEADS, 1), jnp.float32)}
    _L3_gnn_all = _L3_gnn_setup()
    _L3_gnn_in = {k: v for k, v in _L3_gnn_all.items() if k in ('W1', 'b1', 'W2', 'b2', 'A1', 'ab1', 'A2', 'ab2')}
    del _L3_gnn_all
    return {'x': x, 'src': src, 'dst': dst, 'edge_type_64': edge_type_64, 'edge_weight': edge_weight, 'L0_gnn_weight': _L0_gnn_in['weight'], 'L0_gnn_attn_l': _L0_gnn_in['attn_l'], 'L0_gnn_attn_r': _L0_gnn_in['attn_r'], 'L1_gnn_W1': _L1_gnn_in['W1'], 'L1_gnn_b1': _L1_gnn_in['b1'], 'L1_gnn_W2': _L1_gnn_in['W2'], 'L1_gnn_b2': _L1_gnn_in['b2'], 'L2_gnn_query_emb': _L2_gnn_in['query_emb'], 'L2_gnn_Wq': _L2_gnn_in['Wq'], 'L2_gnn_bq': _L2_gnn_in['bq'], 'L2_gnn_Wk': _L2_gnn_in['Wk'], 'L2_gnn_bk': _L2_gnn_in['bk'], 'L2_gnn_Wv': _L2_gnn_in['Wv'], 'L2_gnn_bv': _L2_gnn_in['bv'], 'L2_gnn_rel_w': _L2_gnn_in['rel_w'], 'L2_gnn_Wo': _L2_gnn_in['Wo'], 'L2_gnn_bo': _L2_gnn_in['bo'], 'L2_gnn_gamma': _L2_gnn_in['gamma'], 'L2_gnn_beta': _L2_gnn_in['beta'], 'L3_gnn_W1': _L3_gnn_in['W1'], 'L3_gnn_b1': _L3_gnn_in['b1'], 'L3_gnn_W2': _L3_gnn_in['W2'], 'L3_gnn_b2': _L3_gnn_in['b2'], 'L3_gnn_A1': _L3_gnn_in['A1'], 'L3_gnn_ab1': _L3_gnn_in['ab1'], 'L3_gnn_A2': _L3_gnn_in['A2'], 'L3_gnn_ab2': _L3_gnn_in['ab2']}

def reference(x, src, dst, edge_type_64, edge_weight, L0_gnn_weight, L0_gnn_attn_l, L0_gnn_attn_r, L1_gnn_W1, L1_gnn_b1, L1_gnn_W2, L1_gnn_b2, L2_gnn_query_emb, L2_gnn_Wq, L2_gnn_bq, L2_gnn_Wk, L2_gnn_bk, L2_gnn_Wv, L2_gnn_bv, L2_gnn_rel_w, L2_gnn_Wo, L2_gnn_bo, L2_gnn_gamma, L2_gnn_beta, L3_gnn_W1, L3_gnn_b1, L3_gnn_W2, L3_gnn_b2, L3_gnn_A1, L3_gnn_ab1, L3_gnn_A2, L3_gnn_ab2):
    import jax
    import jax.numpy as jnp

    def _L0_gnn_ref(x, edge_index, weight, attn_l, attn_r):
        import jax, jax.numpy as jnp
        import numpy as np
        N, IN_CH, HEADS, OUT_CH, E = (50000, 256, 4, 64, 25000)
        heads, out_ch = attn_l.shape
        n = x.shape[0]
        xt = jnp.matmul(x, weight).reshape(-1, heads, out_ch)
        row, col = (edge_index[0], edge_index[1])
        alpha_l = jnp.einsum('ehd,hd->eh', xt[row], attn_l)
        alpha_r = jnp.einsum('ehd,hd->eh', xt[col], attn_r)
        alpha = jax.nn.softmax(jax.nn.leaky_relu(alpha_l + alpha_r, 0.01), axis=1)
        tmp = jnp.einsum('nh,nhd->nd', alpha[:n], xt[col[:n]])
        out = jnp.broadcast_to(tmp[:, None, :], (n, heads, out_ch))
        return out.reshape(n, heads * out_ch)

    def _L1_gnn_ref(x, W1, b1, W2, b2, edge_index):
        import jax, jax.numpy as jnp
        import numpy as np
        N, E, D_IN, D_OUT = (50000, 50000, 256, 256)
        dst = edge_index[0]
        nbr = edge_index[1]
        n = x.shape[0]
        agg = jax.ops.segment_sum(x[nbr], dst, num_segments=n)
        cnt = jax.ops.segment_sum(jnp.ones((nbr.shape[0],), x.dtype), dst, num_segments=n)
        mean = agg / jnp.maximum(cnt, 1.0)[:, None]
        return x @ W1.T + b1 + mean @ W2.T + b2

    def _L2_gnn_ref(node_features, edge_index, edge_relations, query_emb, Wq, bq, Wk, bk, Wv, bv, rel_w, Wo, bo, gamma, beta):
        import jax, jax.numpy as jnp
        import numpy as np
        N_NODES = 50000
        N_EDGES = 15625
        IN_DIM = 256
        HID = 64
        HEADS = 4
        N_REL = 64
        N = node_features.shape[0]
        D = rel_w.shape[1]
        H = Wq.shape[1] // D
        enh = node_features + 0.1 * query_emb[None, :]
        Q = (enh @ Wq + bq).reshape(N, H, D)
        K = (enh @ Wk + bk).reshape(N, H, D)
        V = (enh @ Wv + bv).reshape(N, H, D)
        src, dst = (edge_index[0], edge_index[1])
        rel = rel_w[edge_relations]
        mod_k = K[src] + 0.2 * rel[:, None, :]
        scores = jnp.einsum('ehd,ehd->eh', Q[dst], mod_k) / D ** 0.5
        seg_max = jax.ops.segment_max(scores, dst, num_segments=N)
        ex = jnp.exp(scores - seg_max[dst])
        denom = jax.ops.segment_sum(ex, dst, num_segments=N)
        w = ex / denom[dst]
        agg = jax.ops.segment_sum(w[:, :, None] * V[src], dst, num_segments=N)
        deg = jax.ops.segment_sum(jnp.ones((src.shape[0],), jnp.float32), dst, num_segments=N)
        msgs = jnp.where(deg[:, None, None] > 0, agg, V)
        out = msgs.reshape(N, H * D) @ Wo + bo
        x = out + node_features
        mu = jnp.mean(x, axis=-1, keepdims=True)
        var = jnp.var(x, axis=-1, keepdims=True)
        return (x - mu) / jnp.sqrt(var + 1e-05) * gamma + beta

    def _L3_gnn_ref(x, idx, elem, W1, b1, W2, b2, A1, ab1, A2, ab2):
        import jax, jax.numpy as jnp
        import numpy as np
        N_NODES = 50000
        N_EDGES = 25000
        IN_DIM, HID_DIM, OUT_DIM, N_HEADS = (256, 256, 64, 4)
        ATT_DIM = OUT_DIM * 2 + 1
        row, col = (idx[0], idx[1])
        n = x.shape[0]

        def head(w1, bb1, w2, bb2, a1, aab1, a2, aab2):
            feats = jnp.maximum(x @ w1 + bb1, 0.0) @ w2 + bb2
            x_cat = jnp.concatenate([feats[row], feats[col], elem[:, None]], axis=1)
            hid = jnp.maximum(x_cat @ a1 + aab1, 0.0)
            e1 = (hid @ a2 + aab2)[:, 0]
            e1 = jax.nn.leaky_relu(e1, negative_slope=0.2)
            w = jnp.exp(e1 - jnp.max(e1))
            pooled = jax.ops.segment_sum(w[:, None] * feats[col], row, num_segments=n)
            row_sum = jax.ops.segment_sum(w, row, num_segments=n) + 1e-10
            return pooled / row_sum[:, None]
        h = jax.vmap(head)(W1, b1, W2, b2, A1, ab1, A2, ab2)
        return jnp.transpose(h, (1, 0, 2)).reshape(n, -1)
    edge_index = jnp.stack([src, dst])
    h = jnp.maximum(_layernorm(x, axis=-1), 0.0)
    x = x + _L0_gnn_ref(h, edge_index, L0_gnn_weight, L0_gnn_attn_l, L0_gnn_attn_r)
    h = jnp.maximum(_layernorm(x, axis=-1), 0.0)
    x = x + _L1_gnn_ref(h, L1_gnn_W1, L1_gnn_b1, L1_gnn_W2, L1_gnn_b2, edge_index)
    h = jnp.maximum(_layernorm(x, axis=-1), 0.0)
    x = x + _L2_gnn_ref(h, edge_index, edge_type_64, L2_gnn_query_emb, L2_gnn_Wq, L2_gnn_bq, L2_gnn_Wk, L2_gnn_bk, L2_gnn_Wv, L2_gnn_bv, L2_gnn_rel_w, L2_gnn_Wo, L2_gnn_bo, L2_gnn_gamma, L2_gnn_beta)
    h = jnp.maximum(_layernorm(x, axis=-1), 0.0)
    x = x + _L3_gnn_ref(h, edge_index, edge_weight, L3_gnn_W1, L3_gnn_b1, L3_gnn_W2, L3_gnn_b2, L3_gnn_A1, L3_gnn_ab1, L3_gnn_A2, L3_gnn_ab2)
    return x

_drawn_inputs = setup_inputs


def setup_inputs(seed=0):
    import zlib

    import numpy as np

    out = dict(_drawn_inputs(seed))
    spreads = {'L2_gnn_bq': (0.0, 2.0),
     'L2_gnn_bk': (0.0, 2.0),
     'L2_gnn_bv': (0.0, 0.304),
     'L2_gnn_bo': (0.0, 0.1),
     'L2_gnn_gamma': (1.0, 0.2),
     'L2_gnn_beta': (0.0, 0.1),
     'L3_gnn_b1': (0.0, 0.391),
     'L3_gnn_b2': (0.0, 0.1),
     'L3_gnn_ab1': (0.0, 2.0),
     'L3_gnn_ab2': (0.0, 2.0)}
    factors = {'edge_weight': 8.0,
     'L2_gnn_query_emb': 7.859,
     'L2_gnn_Wq': 8.0,
     'L2_gnn_Wk': 8.0,
     'L2_gnn_rel_w': 200.0,
     'L3_gnn_A1': 8.0,
     'L3_gnn_A2': 8.0}
    for name, (base, spread) in spreads.items():
        noise = np.random.default_rng([zlib.crc32(name.encode()), seed]).standard_normal(out[name].shape)
        drawn = base * np.exp(spread * noise) if base else spread * noise
        out[name] = jnp.asarray(drawn.astype(out[name].dtype))
    for name, factor in factors.items():
        out[name] = (out[name] * factor).astype(out[name].dtype)
    return out
```

```python
from contextlib import ExitStack

import concourse.bass as bass
from concourse import mybir

ALU = mybir.AluOpType
ACT = mybir.ActivationFunctionType
AX = mybir.AxisListType
F32 = mybir.dt.float32
BF16 = mybir.dt.bfloat16
I32 = mybir.dt.int32

N = 3125
D = 256
E = 53125
H = 4
HD = 64
NB = 25
NR = 125
REL = 64
ATT = 2 * HD + 1
HA = H * ATT

EC = 416
ELAST = E - 127 * EC
NKEY = NB + 1
UT = 2
NU = (E + NB * (128 * UT - 1)) // (128 * UT)
RING = 4
AHEAD = 3
NT = UT * (NU + 1 + AHEAD)
NIT = NU // RING
assert NU % RING == 0
NOBODY = 200.0
RW = 4
GROUP = 8
TG = 5
BIG = 2.0 ** 100


class Steps:

    def __init__(self, eng, sem):
        self.eng, self.sem, self.n, self.i, self.per, self.inner = eng, sem, 0, None, 0, 0

    def __call__(self, ins):
        ins.then_inc(self.sem, 1)
        if self.i is None:
            self.n += 1
            self.eng.wait_ge(self.sem, self.n)
        else:
            self.inner += 1
            self.eng.wait_ge(self.sem, self.i * self.per + (self.n + self.inner))

    def enter(self, i, per):
        self.i, self.per, self.inner = i, per, 0

    def leave(self, count):
        assert self.inner == self.per, (self.inner, self.per)
        self.i, self.n = None, self.n + count * self.per


class Phase:

    def __init__(self, nc, name):
        self.nc, self.name, self.ctx, self.sems = nc, name, ExitStack(), []

    def __enter__(self):
        self.ctx.__enter__()
        return self

    def sb(self, name, shape, dt=F32):
        return self.ctx.enter_context(self.nc.sbuf_tensor(f"{self.name}_{name}", shape, dt))

    def psum(self, name, shape, dt=F32):
        return self.ctx.enter_context(self.nc.psum_tensor(f"{self.name}_{name}", shape, dt))

    def sem(self, name):
        self.sems.append(self.nc.alloc_semaphore(f"{self.name}_{name}"))
        return self.sems[-1]

    def __exit__(self, *error):
        left = self.ctx.__exit__(*error)
        if error[0] is None and self.sems:
            self.nc.clear_and_free_semaphores(self.sems)
            self.nc.all_engine_barrier()
        return left


def at(i, k, c):
    return i * k + c


def bcast_rows(vec, rows):
    return vec.rearrange("(a d) -> a d", a=1).to_broadcast([rows, vec.shape[0]])


def wide(a):
    return a.unsqueeze(2).to_broadcast([NR, NB, D])


def center(step, x, out, square, stats, var_ready):
    dve = step.eng
    step(dve.tensor_reduce(stats[:, 0, :], x, AX.X, ALU.add))
    step(dve.tensor_scalar(stats[:, 0, :], stats[:, 0, :], 1.0 / D, None, ALU.mult))
    step(dve.tensor_tensor(out, x, wide(stats[:, 0, :]), ALU.subtract))
    step(dve.tensor_tensor(square, out, out, ALU.mult))
    step(dve.tensor_reduce(stats[:, 1, :], square, AX.X, ALU.add))
    dve.tensor_scalar(stats[:, 1, :], stats[:, 1, :], 1.0 / D, 1e-5, ALU.mult, ALU.add).then_inc(var_ready, 1)


def tile_slot(ps, j):
    return ps[:, j % ps.shape[1], 0:256]


def since(ps, j, count):
    banks = ps.shape[1]
    return banks if j >= banks else min(count - k + j for k in range(count) if k % banks == j)


def each_round(eng, rounds, body):
    body(0)
    with eng.Fori(1, rounds) as i:
        body(i)


def wait_for(eng, sem, value):
    if not isinstance(value, int) or value > 0:
        eng.wait_ge(sem, value)


def stage_indices(act, index, slots, got, staged):
    def body(i):
        for k in range(RING):
            wait_for(act, got[k], at(i, 16 * UT, 0))
            act.copy(slots[:, k, :], index[:, bass.ds((i * RING + k) * UT, UT)]).then_inc(staged, 1)
    each_round(act, NIT, body)


def in_slots(i, k, ahead):
    return i * RING + (k + ahead), (k + ahead) % RING


def stage_ahead(act, index, slots, got, staged, i, k, ahead=AHEAD):
    u, slot = in_slots(i, k, ahead)
    wait_for(act, got[slot], at(i, 16 * UT, (k + ahead) // RING * 16 * UT))
    act.copy(slots[:, slot, :], index[:, bass.ds(u * UT, UT)]).then_inc(staged, 1)


def gather_rows(pool, table, slots, rows, got, staged, apart, freed):
    def body(i):
        for k in range(RING):
            pool.wait_ge(staged, at(i, RING, k + 1))
            wait_for(pool, freed, at(i, RING, k + 1 - RING))
            pool.sem_inc(apart, 1)
            for j in range(UT):
                pool.indirect_dma_start(rows(k, j), None, table,
                                        bass.IndirectOffsetOnAxis(ap=slots[:, k, j:j + 1], axis=0)).then_inc(got[k], 16)
    each_round(pool, NIT, body)


def turned_tile(ps, j):
    return tile_slot(ps, j)[:, 0:2 * NR].rearrange("p (k n) -> p k n", k=2)


def turn_and_multiply(pe, slots, ident, ps_turned, turned_slots, weights, ps_product, sems):
    filled, turned, turned_taken, multiplied, product_taken = sems
    nw = len(weights)
    for s in (turned, turned_taken):
        pe.sem_inc(s, TG)
    for s in (multiplied, product_taken):
        pe.sem_inc(s, TG * nw)
    with pe.Fori(0, NB // TG) as g:
        for j in range(TG):
            pe.wait_ge(filled, at(g, TG, j + 1))
            pe.wait_ge(turned_taken, at(g, TG, TG + j + 1 - since(ps_turned, j, TG)))
            for k in range(2):
                last = pe.transpose(tile_slot(ps_turned, j)[:, k * NR:(k + 1) * NR],
                                    slots[:, j, k * 128:(k + 1) * 128], ident[0:NR, 0:NR])
            last.then_inc(turned, 1)
        for j in range(TG):
            pe.wait_ge(turned_taken, at(g, TG, TG + j + 1))
            for m in range(nw):
                p = j * nw + m
                pe.wait_ge(product_taken, at(g, TG * nw, TG * nw + p + 1 - since(ps_product, p, TG * nw)))
                for k in range(2):
                    last = pe.matmul(tile_slot(ps_product, p)[0:NR, :], turned_slots[:, j, k, :], weights[m][:, k, :],
                                     start=(k == 0), stop=(k == 1))
                last.then_inc(multiplied, 1)


def feed_products(dve, fill, take, slots, ps_turned, turned_slots, ps_product, sems, nw=1):
    filled, turned, turned_taken, multiplied, product_taken = sems
    with dve.Fori(0, NB // TG) as g:
        for j in range(TG):
            dve.wait_ge(turned, at(g, TG, j + 1))
            fill(g * TG + j, slots[:, j, :]).then_inc(filled, 1)
        for j in range(TG):
            dve.wait_ge(turned, at(g, TG, TG + j + 1))
            dve.wait_ge(multiplied, at(g, TG * nw, (j + 1) * nw))
            dve.tensor_copy(turned_slots[:, j, :, :], turned_tile(ps_turned, j)).then_inc(turned_taken, 1)
        for p in range(TG * nw):
            dve.wait_ge(multiplied, at(g, TG * nw, TG * nw + p + 1))
            take(g * TG + p // nw, p % nw, tile_slot(ps_product, p)[0:NR, :]).then_inc(product_taken, 1)
    dve.wait_ge(product_taken, (NB + TG) * nw)


def select_nodes(dve, out, iota, record, tile):
    return dve.tensor_scalar(out, iota[:, 0:out.shape[1]], record[:, bass.ds(tile, 1), 1], None, ALU.is_equal)


def add_unit(dve, i, k, acc, sums, bucket, summed, added):
    dve.wait_ge(summed, at(i, RING, k + 1))
    wait_for(dve, added, at(i, RING, k))
    b = dve.value_load(bucket[0:1, bass.ds(i * RING + k, 1)], min_val=0, max_val=NB - 1)
    dve.tensor_tensor(acc[:, bass.ds(b, 1), :], acc[:, bass.ds(b, 1), :], sums.unsqueeze(1), ALU.add).then_inc(added, 1)


def make_program(nc, t, out, upto=4):
    rec_src = nc.dram_tensor("rec_src", (128 * NT, RW), F32).ap()
    rec_dst = nc.dram_tensor("rec_dst", (128 * NT, RW), F32).ap()
    top = ExitStack()
    with top:
        c = {}
        c["x"] = top.enter_context(nc.sbuf_tensor("x_nodes", [NR, NB, D], F32))
        c["iota"] = top.enter_context(nc.sbuf_tensor("iota", [128, 256], F32))
        c["row"] = top.enter_context(nc.sbuf_tensor("row", [128, 1], F32))
        c["ident"] = top.enter_context(nc.sbuf_tensor("ident", [128, 128], F32))
        c["bucket"] = top.enter_context(nc.sbuf_tensor("bucket", [128, 2, NU + AHEAD], I32))
        sort_edges_and_layer_0(nc, t, c, rec_src, rec_dst)
        c["record"] = top.enter_context(nc.sbuf_tensor("edge_records", [128, 2, NT, RW], F32))
        c["other"] = top.enter_context(nc.sbuf_tensor("edge_others", [128, 2, NT], I32))
        layer_1(nc, t, c, rec_src, rec_dst)
        layer_2(nc, t, c)
        layer_3(nc, t, c)
        with nc.semaphore("out_stored") as out_stored, nc.Block() as block:
            @block.sync
            def _(sp):
                sp.dma_start(out.rearrange("(p b) d -> p b d", b=NB), c["x"][:]).then_inc(out_stored, 16)
                sp.wait_ge(out_stored, 16)


def sort_edges_and_layer_0(nc, t, c, rec_src, rec_dst):
    with Phase(nc, "sort") as phase:
        sb, sem = phase.sb, phase.sem

        iota, row, ident, bucket = c["iota"], c["row"], c["ident"], c["bucket"]
        edges_i = sb("edges_i", [128, 3, EC], I32)
        weight = sb("weight", [128, EC])
        other = sb("other", [128, 3, EC])
        blank = sb("blank", [128, NT, RW])
        before = sb("before", [128, 128])
        ones = sb("ones", [128, 128])
        arena = sb("arena", [128, 2 * NKEY * EC])
        mask = arena[:, 0:NKEY * EC].rearrange("p (b e) -> p b e", b=NKEY)
        count = arena[:, NKEY * EC:2 * NKEY * EC].rearrange("p (b e) -> p b e", b=NKEY)
        WX = D + H
        h = arena[0:NR, 0:NB * D].rearrange("p (b d) -> p b d", b=NB)
        xt = arena[0:NR, 2 * NB * WX:3 * NB * WX].rearrange("p (b d) -> p b d", b=NB)
        picked = arena[0:NR, 0:NB * WX].rearrange("p (b d) -> p b d", b=NB)
        tab_right = nc.dram_tensor("tab_right", (N, WX), F32).ap()
        tab_left = nc.dram_tensor("tab_left", (N, H), F32).ap()
        h_slots = sb("h_slots", [NR, TG, D])
        turned_slots = sb("turned_slots", [128, TG, 2, NR])
        w0 = sb("w0", [128, 2, D])
        attn = sb("attn", [NR, 2, D])
        left = sb("left", [NR, NB, H])
        picked_left = sb("picked_left", [NR, NB, H])
        row_idx = sb("row_idx", [NR, 2, NB], I32)
        alpha = sb("alpha", [NR, 2, NB, H])
        alpha_1 = sb("alpha_1", [NR, NB])
        stats = sb("stats", [NR, 3, NB])
        junk = sb("junk", [NR, D])
        quot = sb("quot", [128, EC])
        quot_i = sb("quot_i", [128, EC], I32)
        rem = sb("rem", [128, EC])
        flag = sb("flag", [128, EC])
        place = sb("place", [128, 2, EC])
        record = sb("record", [128, 2, EC, RW])
        small = sb("small", [128, 8, NKEY])
        small_i = sb("small_i", [128, 2, NKEY], I32)
        reach = sb("reach", [128, NU + AHEAD, NB - 1])
        reached = sb("reached", [128, NU + AHEAD])
        slot_i = sb("slot_i", [128, 2, GROUP], I32)
        slot_rec = sb("slot_rec", [128, 2, GROUP, RW])
        ps = phase.psum("ps_counts", [128, 512], F32)
        ps_turned = phase.psum("ps_turned", [128, 4, 512], F32)
        ps_product = phase.psum("ps_product", [128, 3, 512], F32)

        loaded = sem("loaded")
        made = sem("made")
        blanked = sem("blanked")
        dstep = sem("dstep")
        const_ready = sem("const_ready")
        counts_ready = sem("counts_ready")
        sums_ready = sem("sums_ready")
        prefilled = sem("prefilled")
        sorted_ = sem("sorted_")
        w0_loaded = sem("w0_loaded")
        std_ready = sem("std_ready")
        astep = sem("astep")
        filled = sem("filled")
        turned = sem("turned")
        turned_taken = sem("turned_taken")
        multiplied = sem("multiplied")
        product_taken = sem("product_taken")
        tables_ready = sem("tables_ready")
        tables_stored = sem("tables_stored")
        picked_ready = sem("picked_ready")
        logits_ready = sem("logits_ready")
        exps_ready = sem("exps_ready")
        staged = sem("staged")
        taken = sem("taken")
        group_done = [sem(f"group_done{g}") for g in range(2)]
        block = phase.ctx.enter_context(nc.Block())

        @block.sync
        def _(sp):
            sp.dma_start(c["x"][:], t["x"].rearrange("(p b) d -> p b d", b=NB)).then_inc(loaded, 16)
            sp.wait_ge(blanked, 1)
            for k, name in enumerate(("src", "dst", "edge_type_64")):
                a = t[name]
                sp.dma_start(edges_i[0:127, k, :], a[0:127 * EC].rearrange("(p e) -> p e", e=EC)).then_inc(loaded, 16)
                sp.dma_start(edges_i[127:128, k, 0:ELAST], a[127 * EC:E].rearrange("(p e) -> p e", p=1)).then_inc(loaded, 16)
            a = t["edge_weight"]
            sp.dma_start(weight[0:127, :], a[0:127 * EC].rearrange("(p e) -> p e", e=EC)).then_inc(loaded, 16)
            sp.dma_start(weight[127:128, 0:ELAST], a[127 * EC:E].rearrange("(p e) -> p e", p=1)).then_inc(loaded, 16)
            sp.wait_ge(blanked, 2)
            for rec in (rec_src, rec_dst):
                sp.dma_start(rec.rearrange("(l t) w -> l t w", t=NT), blank[:]).then_inc(prefilled, 16)
            sp.dma_start(w0[:], t["L0_gnn_weight"].rearrange("(k p) d -> p k d", p=128)).then_inc(w0_loaded, 16)
            for k, name in enumerate(("L0_gnn_attn_l", "L0_gnn_attn_r")):
                sp.dma_start(attn[:, k, :], bcast_rows(t[name].rearrange("h d -> (h d)"), NR)).then_inc(w0_loaded, 16)
            for k, name in enumerate(("src", "dst")):
                sp.dma_start(row_idx[:, k, :], t[name][0:N].rearrange("(p b) -> p b", b=NB)).then_inc(w0_loaded, 16)
            sp.wait_ge(tables_ready, 1)
            sp.dma_start(tab_right.rearrange("(p b) d -> p b d", b=NB), xt).then_inc(tables_stored, 16)
            sp.dma_start(tab_left.rearrange("(p b) d -> p b d", b=NB), left[:]).then_inc(tables_stored, 16)

        @block.gpsimd
        def _(pool):
            pool.iota(iota[:], [[1, 256]], base=0, channel_multiplier=0,
                      allow_small_or_imprecise_dtypes=True)
            pool.iota(row[:], [[0, 1]], base=0, channel_multiplier=1,
                      allow_small_or_imprecise_dtypes=True).then_inc(made, 1)
            pool.wait_ge(prefilled, 32)
            for o, rec in enumerate((rec_src, rec_dst)):
                with pool.Fori(0, EC // (2 * GROUP)) as i:
                    for g in range(2):
                        pool.wait_ge(staged, at(i, 2, o * (EC // GROUP) + g + 1))
                        pool.sem_inc(taken, 1)
                        for k in range(GROUP):
                            pool.indirect_dma_start(
                                rec, bass.IndirectOffsetOnAxis(ap=slot_i[:, g, k:k + 1], axis=0),
                                slot_rec[:, g, k, :], None).then_inc(group_done[g], 16)
                if o == 0:
                    pool.wait_ge(tables_stored, 32)
                    pool.wait_ge(w0_loaded, 16 * 5)
                    for b in range(NB):
                        pool.indirect_dma_start(picked[:, b, :], None, tab_right, bass.IndirectOffsetOnAxis(
                            ap=row_idx[:, 1, b:b + 1], axis=0)).then_inc(picked_ready, 16)
                        pool.indirect_dma_start(picked_left[:, b, :], None, tab_left, bass.IndirectOffsetOnAxis(
                            ap=row_idx[:, 0, b:b + 1], axis=0)).then_inc(picked_ready, 16)
            for g in range(2):
                pool.wait_ge(group_done[g], EC * 16)

        @block.tensor
        def _(pe):
            for o in range(2):
                pe.wait_ge(counts_ready, o + 1)
                pe.matmul(ps[:, 0:NKEY], before[:], small[:, 2, :], start=True, stop=True)
                pe.matmul(ps[:, 32:32 + NKEY], ones[:], small[:, 2, :], start=True, stop=True).then_inc(sums_ready, 1)
            pe.wait_ge(w0_loaded, 16 * 5)
            turn_and_multiply(pe, h_slots, ident, ps_turned, turned_slots, [w0], ps_product,
                              (filled, turned, turned_taken, multiplied, product_taken))

        @block.vector
        def _(dve):
            step = Steps(dve, dstep)
            dve.memset(other[:, 2, :], 0.0)
            for k, fill in ((0, N), (1, N), (2, 0)):
                dve.memset(edges_i[:, k, :], fill)
            dve.memset(weight[:], 0.0).then_inc(blanked, 1)
            step(dve.memset(blank[:], 0.0))
            dve.memset(blank[:, :, 1], NOBODY).then_inc(blanked, 1)
            dve.memset(ones[:], 1.0)
            step(dve.memset(record[:], 0.0))
            dve.wait_ge(made, 1)
            dve.tensor_scalar(ident[:], iota[:, 0:128], row[:, 0:1], None, ALU.is_equal)
            step(dve.tensor_scalar(before[:], iota[:, 0:128], row[:, 0:1], None, ALU.is_gt))
            dve.wait_ge(loaded, 16 * 9)
            step(dve.tensor_copy(other[:], edges_i[:]))
            for o in range(2):
                key = other[:, o, :]
                step(dve.tensor_scalar(quot_i[:], key, 1.0 / NB, None, ALU.mult))
                step(dve.tensor_copy(quot[:], quot_i[:]))
                step(dve.scalar_tensor_tensor(rem[:], quot[:], -float(NB), key, ALU.mult, ALU.add))
                step(dve.tensor_scalar(flag[:], rem[:], 0.0, None, ALU.is_lt))
                step(dve.tensor_tensor(quot[:], quot[:], flag[:], ALU.subtract))
                step(dve.scalar_tensor_tensor(rem[:], flag[:], float(NB), rem[:], ALU.mult, ALU.add))
                step(dve.tensor_scalar(flag[:], rem[:], float(NB), None, ALU.is_ge))
                step(dve.tensor_tensor(quot[:], quot[:], flag[:], ALU.add))
                step(dve.scalar_tensor_tensor(rem[:], flag[:], -float(NB), rem[:], ALU.mult, ALU.add))
                step(dve.tensor_scalar(flag[:], key, float(N), None, ALU.is_ge))
                step(dve.scalar_tensor_tensor(rem[:], flag[:], float(NB), rem[:], ALU.mult, ALU.add))
                step(dve.scalar_tensor_tensor(quot[:], flag[:], NOBODY - NR, quot[:], ALU.mult, ALU.add))
                step(dve.tensor_scalar(flag[:], other[:, 1 - o, :], float(N), None, ALU.is_lt))
                dve.tensor_tensor(record[:, o, :, 0], flag[:], other[:, 1 - o, :], ALU.mult)
                dve.tensor_copy(record[:, o, :, 1], quot[:])
                step(dve.tensor_copy(record[:, o, :, 2], weight[:] if o == 0 else other[:, 2, :]))
                step(dve.tensor_tensor(mask, rem[:].unsqueeze(1).to_broadcast([128, NKEY, EC]),
                                       iota[:, 0:NKEY].unsqueeze(2).to_broadcast([128, NKEY, EC]), ALU.is_equal))
                m = mask.rearrange("p b e -> p (b e)")
                step(dve.tensor_tensor_scan(count.rearrange("p b e -> p (b e)"), m, m, 0.0, ALU.add, ALU.max))
                earlier, here, mine, units, end, start, off, total = (small[:, k, :] for k in range(8))
                dve.memset(small[:, 0, 0:1], 0.0)
                step(dve.tensor_copy(small[:, 0, 1:NKEY], count[:, 0:NKEY - 1, EC - 1]))
                dve.tensor_tensor(mine, count[:, :, EC - 1], earlier, ALU.subtract).then_inc(counts_ready, 1)
                dve.wait_ge(sums_ready, o + 1)
                step(dve.tensor_scalar(small_i[:, 0, :], ps[:, 32:32 + NKEY], float(128 * UT - 1), None, ALU.add))
                step(dve.tensor_scalar(small_i[:, 1, :], small_i[:, 0, :], 7 + UT // 2, None, ALU.arith_shift_right))
                step(dve.tensor_copy(units, small_i[:, 1, :]))
                step(dve.tensor_tensor_scan(end, units, units, 0.0, ALU.add, ALU.max))
                step(dve.tensor_tensor(start, end, units, ALU.subtract))
                step(dve.tensor_tensor(off, ps[:, 0:NKEY], earlier, ALU.subtract))
                step(dve.scalar_tensor_tensor(off, start, float(128 * UT), off, ALU.mult, ALU.add))
                step(dve.tensor_scalar(off, off, -1.0, None, ALU.add))
                step(dve.tensor_tensor(count, count, off.unsqueeze(2).to_broadcast([128, NKEY, EC]), ALU.add))
                step(dve.tensor_tensor(count, count, mask, ALU.mult))
                step(dve.tensor_reduce(rem[:], count.rearrange("p b e -> p e b"), AX.X, ALU.add))
                step(dve.tensor_copy(quot_i[:], rem[:]))
                step(dve.tensor_scalar(quot_i[:], quot_i[:], 7, None, ALU.arith_shift_right))
                step(dve.tensor_copy(quot[:], quot_i[:]))
                step(dve.scalar_tensor_tensor(rem[:], quot[:], -128.0, rem[:], ALU.mult, ALU.add))
                step(dve.scalar_tensor_tensor(place[:, o, :], rem[:], float(NT), quot[:], ALU.mult, ALU.add))
                step(dve.tensor_tensor(reach[:], iota[:, 0:NU + AHEAD].unsqueeze(2).to_broadcast([128, NU + AHEAD, NB - 1]),
                                       small[:, 5, 1:NB].unsqueeze(1).to_broadcast([128, NU + AHEAD, NB - 1]), ALU.is_ge))
                step(dve.tensor_reduce(reached[:], reach[:], AX.X, ALU.add))
                step(dve.tensor_copy(bucket[:, o, :], reached[:]))
                dve.sem_inc(sorted_, 1)
            dve.wait_ge(std_ready, 1)
            step(dve.reciprocal(stats[:, 2, :], stats[:, 2, :]))
            with dve.Fori(0, NB // TG) as g:
                for j in range(TG):
                    dve.wait_ge(turned, at(g, TG, j + 1))
                    b = g * TG + j
                    dve.tensor_scalar(h_slots[:, j, :], c["x"][:, b, :], stats[:, 0, bass.ds(b, 1)],
                                      stats[:, 2, bass.ds(b, 1)], ALU.add, ALU.mult).then_inc(filled, 1)
                for j in range(TG):
                    dve.wait_ge(turned, at(g, TG, TG + j + 1))
                    dve.wait_ge(multiplied, at(g, TG, j + 1))
                    dve.tensor_scalar(turned_slots[:, j, :, :], turned_tile(ps_turned, j), 0.0, None,
                                      ALU.max).then_inc(turned_taken, 1)
                for j in range(TG):
                    dve.wait_ge(multiplied, at(g, TG, TG + j + 1))
                    dve.tensor_copy(xt[:, g * TG + j, 0:D], tile_slot(ps_product, j)[0:NR, :]).then_inc(product_taken, 1)
            dve.wait_ge(product_taken, NB + TG)
            dve.wait_ge(w0_loaded, 16 * 5)
            for k, to in ((1, xt[:, :, D:WX]), (0, left[:])):
                step(dve.tensor_tensor(h, xt[:, :, 0:D], attn[:, k, :].unsqueeze(1).to_broadcast([NR, NB, D]), ALU.mult))
                step(dve.tensor_reduce(to, h.rearrange("p b (h d) -> p b h d", h=H), AX.X, ALU.add))
            dve.sem_inc(tables_ready, 1)
            dve.wait_ge(picked_ready, 2 * NB * 16)
            logit, prob = alpha[:, 0], alpha[:, 1]
            step(dve.tensor_tensor(logit, picked[:, :, D:WX], picked_left[:], ALU.add))
            step(dve.scalar_tensor_tensor(logit, logit, 0.01, logit, ALU.mult, ALU.max))
            step(dve.tensor_reduce(alpha_1[:], logit, AX.X, ALU.max))
            per_head = alpha_1[:].unsqueeze(2).to_broadcast([NR, NB, H])
            dve.tensor_tensor(logit, logit, per_head, ALU.subtract).then_inc(logits_ready, 1)
            dve.wait_ge(exps_ready, 1)
            step(dve.tensor_reduce(alpha_1[:], prob, AX.X, ALU.add))
            step(dve.reciprocal(alpha_1[:], alpha_1[:]))
            step(dve.tensor_tensor(prob, prob, per_head, ALU.mult))
            mixed = picked[:, :, 0:D].rearrange("p b (h d) -> p b h d", h=H)
            for b in range(NB):
                last = dve.tensor_tensor(mixed[:, b], mixed[:, b], prob[:, b, :].unsqueeze(2).to_broadcast([NR, H, HD]), ALU.mult)
            step(last)
            summed = xt[:, :, 0:HD]
            step(dve.tensor_reduce(summed, picked[:, :, 0:D].rearrange("p b (h d) -> p b d h", h=H), AX.X, ALU.add))
            for k in range(H):
                xk = c["x"][:, :, k * HD:(k + 1) * HD]
                last = dve.tensor_tensor(xk, xk, summed, ALU.add)
            step(last)

        @block.scalar
        def _(act):
            act.wait_ge(loaded, 16 * 9)
            with act.Fori(0, NB) as b:
                act.activation(junk[:], c["x"][:, b, :], ACT.Copy, accum_out=stats[:, 0, bass.ds(b, 1)]).then_inc(astep, 1)
                act.wait_ge(astep, at(b, 1, 1))
            act.mul(stats[:, 0, :], stats[:, 0, :], -1.0 / D).then_inc(astep, 1)
            act.wait_ge(astep, NB + 1)
            with act.Fori(0, NB) as b:
                act.activation(junk[:], c["x"][:, b, :], ACT.Square, bias=stats[:, 0, bass.ds(b, 1)],
                               accum_out=stats[:, 1, bass.ds(b, 1)]).then_inc(astep, 1)
                act.wait_ge(astep, at(b, 1, NB + 2))
            act.activation(stats[:, 1, :], stats[:, 1, :], ACT.Copy, bias=1e-5, scale=1.0 / D).then_inc(astep, 1)
            act.wait_ge(astep, 2 * NB + 2)
            act.activation(stats[:, 2, :], stats[:, 1, :], ACT.Sqrt).then_inc(std_ready, 1)
            for o in range(2):
                if o == 1:
                    act.wait_ge(logits_ready, 1)
                    act.activation(alpha[:, 1], alpha[:, 0], ACT.Exp).then_inc(exps_ready, 1)
                act.wait_ge(sorted_, o + 1)

                def stage(i):
                    for g in range(2):
                        if o or not isinstance(i, int):
                            act.wait_ge(group_done[g], at(i, 16 * GROUP, o * (EC // 2) * 16))
                        cols = bass.ds(i * (2 * GROUP) + g * GROUP, GROUP)
                        act.copy(slot_i[:, g, :], place[:, o, cols])
                        act.copy(slot_rec[:, g, :, :], record[:, o, cols, :]).then_inc(staged, 1)

                if o == 0:
                    stage(0)
                with act.Fori(1 - o, EC // (2 * GROUP)) as i:
                    stage(i)


def layer_1(nc, t, c, rec_src, rec_dst):
    tab_h = nc.dram_tensor("tab_h", (N, D), F32).ap()
    x, iota, ident = c["x"], c["iota"], c["ident"]
    with Phase(nc, "l1") as phase:
        sb, sem = phase.sb, phase.sem

        h = sb("h", [NR, NB, D])
        square = sb("square", [NR, NB, D])
        acc = sb("acc", [NR, NB, D + 1])
        stats = sb("stats", [NR, 3, NB])
        bias = sb("bias", [NR, 2, D])
        w_rows = sb("w_rows", [128, 2, 2, D])
        w = sb("w", [128, 2, 2, D])
        slots = sb("slots", [NR, TG, D])
        turned_slots = sb("turned_slots", [128, TG, 2, NR])
        idx_slot = sb("idx_slot", [128, RING, UT], I32)
        rows = sb("rows", [128, RING, UT, D + 1])
        sel = sb("sel", [128, RING, UT, 128])
        ps = phase.psum("ps", [128, 8, 512], F32)
        ps_turned, ps_product, ps_sum = ps[:, 0:4], ps[:, 4:7], ps[:, 0:4]

        records_loaded, w_loaded, w_turned, w_ready = sem("records_loaded"), sem("w_loaded"), sem("w_turned"), sem("w_ready")
        dstep, var_ready, std_ready, h_ready, h_stored = (sem(n) for n in ("dstep", "var_ready", "std_ready", "h_ready", "h_stored"))
        others_ready = sem("others_ready")
        dense = [[sem(f"{n}{k}") for n in ("filled", "turned", "turned_taken", "multiplied", "product_taken")] for k in range(2)]
        staged, apart, sel_ready, summed, added = (sem(n) for n in ("staged", "apart", "sel_ready", "summed", "added"))
        got = [sem(f"got{k}") for k in range(RING)]
        block = phase.ctx.enter_context(nc.Block())

        @block.sync
        def _(sp):
            for o, rec in enumerate((rec_src, rec_dst)):
                sp.dma_start(c["record"][:, o], rec.rearrange("(l t) w -> l t w", t=NT)).then_inc(records_loaded, 16)
            for k in range(2):
                sp.dma_start(w_rows[:, k], t[f"L1_gnn_W{k + 1}"].rearrange("(c p) d -> p c d", p=128)).then_inc(w_loaded, 16)
                sp.dma_start(bias[:, k, :], bcast_rows(t[f"L1_gnn_b{k + 1}"], NR)).then_inc(w_loaded, 16)
            sp.wait_ge(h_ready, 1)
            sp.dma_start(tab_h.rearrange("(p b) d -> p b d", b=NB), h[:]).then_inc(h_stored, 16)

        @block.scalar
        def _(act):
            act.wait_ge(var_ready, 1)
            act.activation(stats[:, 2, :], stats[:, 1, :], ACT.Sqrt).then_inc(std_ready, 1)
            act.wait_ge(others_ready, 1)
            stage_indices(act, c["other"][:, 0], idx_slot, got, staged)

        @block.gpsimd
        def _(pool):
            pool.wait_ge(h_stored, 16)
            gather_rows(pool, tab_h, idx_slot, lambda k, j: rows[:, k, j, 0:D], got, staged, apart, summed)

        @block.tensor
        def _(pe):
            pe.wait_ge(w_loaded, 64)
            for k in range(2):
                for i in range(2):
                    for o in range(2):
                        last = pe.transpose(ps[:, 2 * k + i, o * 128:(o + 1) * 128],
                                            w_rows[:, k, o, i * 128:(i + 1) * 128], ident[:])
            last.then_inc(w_turned, 1)
            pe.wait_ge(w_ready, 1)
            turn_and_multiply(pe, slots, ident, ps_turned, turned_slots, [w[:, 0]], ps_product, dense[0])
            pe.wait_ge(dense[0][2], NB + TG)

            def body(i):
                for k in range(RING):
                    pe.wait_ge(sel_ready, at(i, RING, k + 1))
                    wait_for(pe, added, at(i, RING, k + 1 - RING))
                    pe.wait_ge(got[k], at(i, 16 * UT, 16 * UT))
                    for j in range(UT):
                        last = pe.matmul(ps_sum[0:NR, k, 0:D + 1], sel[:, k, j, 0:NR], rows[:, k, j, :],
                                         start=(j == 0), stop=(j == UT - 1))
                    last.then_inc(summed, 1)
            each_round(pe, NIT, body)
            pe.wait_ge(added, NU)
            turn_and_multiply(pe, slots, ident, ps_turned, turned_slots, [w[:, 1]], ps_product, dense[1])

        @block.vector
        def _(dve):
            step = Steps(dve, dstep)

            def add_to_x(b, _, product):
                return dve.tensor_tensor(x[:, b, :], x[:, b, :], product, ALU.add)

            dve.memset(rows[:, :, :, D], 1.0)
            step(dve.memset(acc[:], 0.0))
            center(step, x[:], h[:], square[:], stats, var_ready)
            dve.wait_ge(std_ready, 1)
            step(dve.reciprocal(stats[:, 2, :], stats[:, 2, :]))
            step(dve.scalar_tensor_tensor(h[:], h[:], 0.0, wide(stats[:, 2, :]), ALU.max, ALU.mult))
            dve.sem_inc(h_ready, 1)
            dve.wait_ge(records_loaded, 32)
            dve.tensor_copy(c["other"][:], c["record"][:, :, :, 0]).then_inc(others_ready, 1)
            dve.wait_ge(w_turned, 1)
            dve.tensor_copy(w[:].rearrange("p k i d -> p (k i) d"), ps[:, 0:4, 0:D]).then_inc(w_ready, 1)
            step(dve.tensor_tensor(bias[:, 0, :], bias[:, 0, :], bias[:, 1, :], ALU.add))
            step(dve.tensor_tensor(x[:], x[:], bias[:, 0, :].unsqueeze(1).to_broadcast([NR, NB, D]), ALU.add))
            feed_products(dve, lambda b, slot: dve.tensor_copy(slot, h[:, b, :]), add_to_x, slots, ps_turned, turned_slots, ps_product, dense[0])

            def body(i):
                for k in range(RING):
                    wait_for(dve, summed, at(i, RING, k + 1 - RING))
                    for j in range(UT):
                        last = select_nodes(dve, sel[:, k, j, 0:NR], iota, c["record"][:, 0], (i * RING + k) * UT + j)
                    last.then_inc(sel_ready, 1)
                for k in range(RING):
                    add_unit(dve, i, k, acc, ps_sum[0:NR, k, 0:D + 1], c["bucket"][:, 0], summed, added)
            each_round(dve, NIT, body)
            dve.wait_ge(added, NU)
            total = stats[:, 0, :]
            step(dve.tensor_scalar(total, acc[:, :, D], 1.0, None, ALU.max))
            step(dve.reciprocal(total, total))
            step(dve.tensor_tensor(acc[:, :, 0:D], acc[:, :, 0:D], wide(total), ALU.mult))
            feed_products(dve, lambda b, slot: dve.tensor_copy(slot, acc[:, b, 0:D]), add_to_x, slots, ps_turned, turned_slots, ps_product, dense[1])


def layer_2(nc, t, c):
    with Phase(nc, "l2") as phase:
        sb = phase.sb
        b = {}
        b["h"] = sb("h", [NR, NB, D])
        b["v"] = sb("v", [NR, NB, D])
        b["score"] = sb("score", [128, NT, H])
        b["top"] = sb("top", [NR, NB, H])
        b["tab_k"] = nc.dram_tensor("tab_k", (N, D), F32).ap()
        b["tab_v"] = nc.dram_tensor("tab_v", (N, D), F32).ap()
        layer_2_scores(nc, t, c, b)
        layer_2_top(nc, c, b)
        layer_2_values(nc, t, c, b)


def layer_2_scores(nc, t, c, b):
    x, iota, ident = c["x"], c["iota"], c["ident"]
    record, bucket = c["record"][:, 1], c["bucket"][:, 1]
    with Phase(nc, "l2a") as phase:
        sb, sem = phase.sb, phase.sem

        h, v, score = b["h"], b["v"], b["score"]
        q = sb("q", [NR, NB, D])
        k_nodes = sb("k", [NR, NB, D])
        stats = sb("stats", [NR, 3, NB])
        w = sb("w", [128, 3, 2, D])
        bias = sb("bias", [NR, 4, D])
        rel = sb("rel", [REL, HD])
        rel_wide = sb("rel_wide", [REL, H, HD])
        slots = sb("slots", [NR, TG, D])
        turned_slots = sb("turned_slots", [128, TG, 2, NR])
        idx_slot = sb("idx_slot", [128, RING, UT], I32)
        rows = sb("rows", [128, RING, UT, D])
        sel = sb("sel", [128, RING, UT, 256])
        sel_turned = sb("sel_turned", [128, 2, UT, 256])
        q_rows = sb("q_rows", [128, 2, UT, D])
        ps = phase.psum("ps", [128, 8, 512], F32)
        ps_turned, ps_product = ps[:, 0:4], ps[:, 4:7]

        w_loaded, dstep, var_ready, std_ready = (sem(n) for n in ("w_loaded", "dstep", "var_ready", "std_ready"))
        nodes_ready, k_stored, others_ready = sem("nodes_ready"), sem("k_stored"), sem("others_ready")
        dense = [sem(n) for n in ("filled", "turned", "turned_taken", "multiplied", "product_taken")]
        staged, apart, sel_ready, sel_turned_ps, sel_turned_ready = (
            sem(n) for n in ("staged", "apart", "sel_ready", "sel_turned_ps", "sel_turned_ready"))
        keys_ready, q_ready, multiplied, scored = (sem(n) for n in ("keys_ready", "q_ready", "e_multiplied", "scored"))
        got = [sem(f"got{k}") for k in range(RING)]
        block = phase.ctx.enter_context(nc.Block())

        @block.sync
        def _(sp):
            for k, name in enumerate("qkv"):
                sp.dma_start(w[:, k], t[f"L2_gnn_W{name}"].rearrange("(k p) d -> p k d", p=128)).then_inc(w_loaded, 16)
                sp.dma_start(bias[:, k, :], bcast_rows(t[f"L2_gnn_b{name}"], NR)).then_inc(w_loaded, 16)
            sp.dma_start(bias[:, 3, :], bcast_rows(t["L2_gnn_query_emb"], NR)).then_inc(w_loaded, 16)
            sp.dma_start(rel[:], t["L2_gnn_rel_w"]).then_inc(w_loaded, 16)
            sp.wait_ge(nodes_ready, 1)
            sp.dma_start(b["tab_k"].rearrange("(p b) d -> p b d", b=NB), k_nodes[:]).then_inc(k_stored, 16)
            sp.dma_start(b["tab_v"].rearrange("(p b) d -> p b d", b=NB), v[:]).then_inc(k_stored, 16)

        @block.gpsimd
        def _(pool):
            pool.wait_ge(k_stored, 32)
            gather_rows(pool, b["tab_k"], idx_slot, lambda k, j: rows[:, k, j, :], got, staged, apart, keys_ready)

        @block.scalar
        def _(act):
            act.wait_ge(var_ready, 1)
            act.activation(stats[:, 2, :], stats[:, 1, :], ACT.Sqrt).then_inc(std_ready, 1)
            act.wait_ge(others_ready, 1)
            for u in range(AHEAD):
                stage_ahead(act, c["other"][:, 1], idx_slot, got, staged, 0, u, 0)

            def body(i):
                for k in range(RING):
                    stage_ahead(act, c["other"][:, 1], idx_slot, got, staged, i, k)
                    act.wait_ge(sel_turned_ps, at(i, RING, k + 1))
                    wait_for(act, multiplied, at(i, RING, k - 1))
                    act.copy(sel_turned[:, k % 2], ps[:, k % 2].rearrange("p (j n) -> p j n", j=UT)).then_inc(sel_turned_ready, 1)
                    act.wait_ge(multiplied, at(i, RING, k + 1))
                    wait_for(act, scored, at(i, RING, k - 1))
                    act.copy(q_rows[:, k % 2], ps[:, 2 + k % 2].rearrange("p (j d) -> p j d", j=UT)).then_inc(q_ready, 1)
            each_round(act, NIT, body)

        @block.tensor
        def _(pe):
            pe.wait_ge(w_loaded, 128)
            turn_and_multiply(pe, slots, ident, ps_turned, turned_slots, [w[:, k] for k in range(3)], ps_product, dense)
            pe.wait_ge(nodes_ready, 1)

            def turn(i, k, ahead):
                u, slot = in_slots(i, k, ahead)
                pe.wait_ge(sel_ready, at(i, RING, k + ahead + 1))
                wait_for(pe, sel_turned_ready, at(i, RING, k + ahead - 1))
                for j in range(UT):
                    for half in range(2):
                        last = pe.transpose(ps[:, slot % 2, (2 * j + half) * 128:(2 * j + half + 1) * 128],
                                            sel[:, slot, j, half * 128:(half + 1) * 128], ident[:])
                last.then_inc(sel_turned_ps, 1)

            def body(i):
                for k in range(RING):
                    turn(i, k, 1)
                    wait_for(pe, scored, at(i, RING, k - 1))
                    pe.wait_ge(got[k], at(i, 16 * UT, 16 * UT))
                    pe.wait_ge(sel_turned_ready, at(i, RING, k + 1))
                    for j in range(UT):
                        keys = ps[:, 4 + k % 2, j * D:(j + 1) * D]
                        pe.matmul(keys, ident[:], rows[:, k, j, :], start=True, stop=False)
                        last = pe.matmul(keys, sel_turned[0:REL, k % 2, j, 128:256],
                                         rel_wide[:].rearrange("r h d -> r (h d)"), start=False, stop=True)
                    last.then_inc(keys_ready, 1)
                    wait_for(pe, q_ready, at(i, RING, k - 1))
                    node_tile = pe.value_load(bucket[0:1, bass.ds(i * RING + k, 1)], min_val=0, max_val=NB - 1)
                    for j in range(UT):
                        last = pe.matmul(ps[:, 2 + k % 2, j * D:(j + 1) * D], sel_turned[0:NR, k % 2, j, 0:128],
                                         q[:, bass.ds(node_tile, 1), :].rearrange("p o d -> p (o d)"), start=True, stop=True)
                    last.then_inc(multiplied, 1)
            turn(0, 0, 0)
            each_round(pe, NIT, body)

        @block.vector
        def _(dve):
            step = Steps(dve, dstep)
            dve.memset(sel[:], 0.0)
            step(dve.memset(score[:], 0.0))
            center(step, x[:], h[:], v[:], stats, var_ready)
            dve.wait_ge(std_ready, 1)
            step(dve.reciprocal(stats[:, 2, :], stats[:, 2, :]))
            step(dve.scalar_tensor_tensor(h[:], h[:], 0.0, wide(stats[:, 2, :]), ALU.max, ALU.mult))
            dve.tensor_copy(c["other"][:, 1], c["record"][:, 1, :, 0]).then_inc(others_ready, 1)
            dve.wait_ge(w_loaded, 128)
            dve.tensor_scalar(rel_wide[:], rel[:].unsqueeze(1).to_broadcast([REL, H, HD]), 0.2, None, ALU.mult)
            step(dve.tensor_scalar(bias[:, 3, :], bias[:, 3, :], 0.1, None, ALU.mult))
            nodes = (q, k_nodes, v)
            feed_products(dve, lambda n, slot: dve.tensor_tensor(slot, h[:, n, :], bias[:, 3, :], ALU.add),
                          lambda n, m, product: dve.tensor_tensor(nodes[m][:, n, :], product, bias[:, m, :], ALU.add),
                          slots, ps_turned, turned_slots, ps_product, dense, nw=3)
            dve.sem_inc(nodes_ready, 1)

            def select(i, k, ahead):
                u, slot = in_slots(i, k, ahead)
                wait_for(dve, sel_turned_ps, at(i, RING, k + ahead + 1 - RING))
                for j in range(UT):
                    tile = u * UT + j
                    dve.tensor_scalar(sel[:, slot, j, 0:NR], iota[:, 0:NR], record[:, bass.ds(tile, 1), 1], None, ALU.is_equal)
                    last = dve.tensor_scalar(sel[:, slot, j, 128:128 + REL], iota[:, 0:REL], record[:, bass.ds(tile, 1), 2], None, ALU.is_equal)
                last.then_inc(sel_ready, 1)

            def body(i):
                for k in range(RING):
                    select(i, k, 2)
                    dve.wait_ge(keys_ready, at(i, RING, k + 1))
                    dve.wait_ge(q_ready, at(i, RING, k + 1))
                    keys = ps[:, 4 + k % 2].rearrange("p (j d) -> p j d", j=UT)
                    dve.tensor_tensor(q_rows[:, k % 2], q_rows[:, k % 2], keys, ALU.mult).then_inc(dstep, 1)
                    dve.wait_ge(dstep, at(i, RING, step.n + k + 1))
                    dve.tensor_reduce(score[:, bass.ds((i * RING + k) * UT, UT), :],
                                      q_rows[:, k % 2].rearrange("p j (h d) -> p (j h) d", h=H), AX.X, ALU.add).then_inc(scored, 1)
            select(0, 0, 0)
            select(0, 1, 0)
            each_round(dve, NIT, body)
            dve.wait_ge(scored, NU)


def layer_2_top(nc, c, b):
    iota, row, ident, score, top = c["iota"], c["row"], c["ident"], b["score"], b["top"]
    record, bucket = c["record"][:, 1], c["bucket"][:, 1]
    parts = 3 * UT * H
    with Phase(nc, "l2b") as phase:
        sb, sem = phase.sb, phase.sem

        rest = sb("rest", [128, NT * H])
        pieces = sb("pieces", [128, NT // UT, 3, UT * H], BF16)
        ident_b = sb("ident_b", [128, 128], BF16)
        pick_1 = sb("pick_1", [parts, UT * H], BF16)
        pick = sb("pick", [parts, UT * H, 128], BF16)
        piece_slot = sb("piece_slot", [128, RING, parts], BF16)
        sel = sb("sel", [128, RING, UT, 128], BF16)
        barred = sb("barred", [128, 2, UT, 128], BF16)
        piece_rows = sb("piece_rows", [parts, 2, 128], BF16)
        unit_top = sb("unit_top", [NR, 2, H])
        negative = sb("negative", [128, 1])
        ps = phase.psum("ps", [128, 4, 512], F32)
        ps_turned = phase.psum("ps_turned", [128, 2, 1024], BF16)
        dstep, sel_ready, turned, rows_ready, laid, topped = (
            sem(n) for n in ("dstep", "sel_ready", "turned", "rows_ready", "laid", "topped"))
        block = phase.ctx.enter_context(nc.Block())

        @block.scalar
        def _(act):
            def body(i):
                for k in range(RING):
                    act.wait_ge(turned, at(i, RING, k + 1))
                    wait_for(act, laid, at(i, RING, k - 1))
                    act.activation(barred[:, k % 2], ps_turned[:, k % 2, 0:UT * 128].rearrange("p (j n) -> p j n", j=UT),
                                   ACT.Identity, bias=negative[:, 0:1], scale=BIG)
                    act.copy(piece_rows[:, k % 2], ps_turned[0:parts, k % 2, UT * 128:(UT + 1) * 128]).then_inc(rows_ready, 1)
            each_round(act, NIT, body)

        @block.tensor
        def _(pe):
            def turn(i, k, ahead):
                u, slot = in_slots(i, k, ahead)
                pe.wait_ge(sel_ready, at(i, RING, k + ahead + 1))
                wait_for(pe, rows_ready, at(i, RING, k + ahead - 1))
                for j in range(UT):
                    pe.transpose(ps_turned[:, slot % 2, j * 128:(j + 1) * 128], sel[:, slot, j, :], ident_b[:])
                pe.transpose(ps_turned[0:parts, slot % 2, UT * 128:(UT + 1) * 128], piece_slot[:, slot, :], ident_b[:]).then_inc(turned, 1)

            def body(i):
                for k in range(RING):
                    turn(i, k, 1)
                    pe.wait_ge(rows_ready, at(i, RING, k + 1))
                    wait_for(pe, topped, at(i, RING, k - 1))
                    for j in range(UT):
                        bank = ps[:, 2 * (k % 2) + j]
                        pe.matmul(bank, ident_b[:], barred[:, k % 2, j, :].unsqueeze(1).to_broadcast([128, H, 128]),
                                  start=True, stop=False)
                        for hd in range(H):
                            last = pe.matmul(bank[:, hd * 128:(hd + 1) * 128], pick[:, j * H + hd, :], piece_rows[:, k % 2],
                                             start=False, stop=(hd == H - 1))
                    last.then_inc(laid, 1)
            turn(0, 0, 0)
            each_round(pe, NIT, body)

        @block.vector
        def _(dve):
            step = Steps(dve, dstep)
            dve.memset(negative[:], -BIG)
            dve.memset(top[:], -BIG)
            dve.tensor_copy(ident_b[:], ident[:])
            step(dve.memset(pick_1[:], 0.0))
            for n in range(3):
                step(dve.scalar_tensor_tensor(pick_1[:], iota[0:parts, n * UT * H:(n + 1) * UT * H], row[0:parts, 0:1],
                                              pick_1[:], ALU.is_equal, ALU.add))
            step(dve.tensor_copy(pick[:], pick_1[:].unsqueeze(2).to_broadcast([parts, UT * H, 128])))
            flat = score[:].rearrange("p t h -> p (t h)").rearrange("p (u k) -> p u k", k=UT * H)
            left = rest[:].rearrange("p (u k) -> p u k", k=UT * H)
            step(dve.tensor_copy(pieces[:, :, 0, :], flat))
            step(dve.tensor_tensor(left, flat, pieces[:, :, 0, :], ALU.subtract))
            step(dve.tensor_copy(pieces[:, :, 1, :], left))
            step(dve.tensor_tensor(left, left, pieces[:, :, 1, :], ALU.subtract))
            step(dve.tensor_copy(pieces[:, :, 2, :], left))

            def select(i, k, ahead):
                u, slot = in_slots(i, k, ahead)
                wait_for(dve, turned, at(i, RING, k + ahead + 1 - RING))
                dve.tensor_copy(piece_slot[:, slot, :], pieces[:, bass.ds(u, 1)].rearrange("p o n k -> p (o n k)"))
                for j in range(UT):
                    last = select_nodes(dve, sel[:, slot, j, :], iota, record, u * UT + j)
                last.then_inc(sel_ready, 1)

            def body(i):
                for k in range(RING):
                    select(i, k, 2)
                    dve.wait_ge(laid, at(i, RING, k + 1))
                    dve.tensor_reduce(unit_top[:, k % 2, :], ps[0:NR, 2 * (k % 2):2 * (k % 2) + 2, :].rearrange(
                        "p j (h e) -> p h j e", h=H), AX.XY, ALU.max).then_inc(dstep, 1)
                    dve.wait_ge(dstep, at(i, RING, step.n + k + 1))
                    wait_for(dve, topped, at(i, RING, k))
                    n = dve.value_load(bucket[0:1, bass.ds(i * RING + k, 1)], min_val=0, max_val=NB - 1)
                    dve.tensor_tensor(top[:, bass.ds(n, 1), :], top[:, bass.ds(n, 1), :], unit_top[:, k % 2, :].unsqueeze(1),
                                      ALU.max).then_inc(topped, 1)
            select(0, 0, 0)
            select(0, 1, 0)
            each_round(dve, NIT, body)
            dve.wait_ge(topped, NU)


def layer_2_values(nc, t, c, b):
    x, iota, ident = c["x"], c["iota"], c["ident"]
    record, bucket = c["record"][:, 1], c["bucket"][:, 1]
    with Phase(nc, "l2c") as phase:
        sb, sem = phase.sb, phase.sem

        h, v, score, top = b["h"], b["v"], b["score"], b["top"]
        acc = sb("acc", [NR, NB, D + H])
        stats = sb("stats", [NR, 3, NB])
        empty = sb("empty", [NR, NB, H])
        wo = sb("wo", [128, 2, D])
        bias = sb("bias", [NR, 3, D])
        slots = sb("slots", [NR, TG, D])
        turned_slots = sb("turned_slots", [128, TG, 2, NR])
        idx_slot = sb("idx_slot", [128, RING, UT], I32)
        rows = sb("rows", [128, RING, UT, D])
        sel = sb("sel", [128, RING, UT, 128])
        sel_turned = sb("sel_turned", [128, 2, UT, 128])
        shifted = sb("shifted", [128, 2, UT, H])
        weighted = sb("weighted", [128, RING, UT, D + H])
        ps = phase.psum("ps", [128, 8, 512], F32)
        ps_turned, ps_product = ps[:, 0:4], ps[:, 4:7]

        w_loaded, dstep, var_ready, std_ready = (sem(n) for n in ("w_loaded", "dstep", "var_ready", "std_ready"))
        dense = [sem(n) for n in ("filled", "turned", "turned_taken", "multiplied", "product_taken")]
        staged, apart, sel_ready, sel_turned_ps, sel_turned_ready = (
            sem(n) for n in ("staged", "apart", "sel_ready", "sel_turned_ps", "sel_turned_ready"))
        top_rows, shifted_ready, exp_ready, weighted_ready, summed, added = (
            sem(n) for n in ("top_rows", "shifted_ready", "exp_ready", "weighted_ready", "summed", "added"))
        got = [sem(f"got{k}") for k in range(RING)]
        block = phase.ctx.enter_context(nc.Block())

        @block.sync
        def _(sp):
            sp.dma_start(wo[:], t["L2_gnn_Wo"].rearrange("(k p) d -> p k d", p=128)).then_inc(w_loaded, 16)
            for k, name in enumerate(("bo", "gamma", "beta")):
                sp.dma_start(bias[:, k, :], bcast_rows(t[f"L2_gnn_{name}"], NR)).then_inc(w_loaded, 16)

        @block.gpsimd
        def _(pool):
            gather_rows(pool, b["tab_v"], idx_slot, lambda k, j: rows[:, k, j, :], got, staged, apart, weighted_ready)

        @block.scalar
        def _(act):
            def take(i, k, ahead):
                u, slot = in_slots(i, k, ahead)
                act.wait_ge(sel_turned_ps, at(i, RING, k + ahead + 1))
                wait_for(act, top_rows, at(i, RING, k + ahead - 1))
                act.copy(sel_turned[:, slot % 2], ps[:, slot % 2, 0:UT * 128].rearrange("p (j n) -> p j n", j=UT)).then_inc(sel_turned_ready, 1)

            def exponentials(i, k, ahead):
                u, slot = in_slots(i, k, ahead)
                act.wait_ge(shifted_ready, at(i, RING, k + ahead + 1))
                wait_for(act, summed, at(i, RING, k + ahead + 1 - RING))
                act.activation(weighted[:, slot, :, D:D + H], shifted[:, slot % 2], ACT.Exp, scale=1.0 / HD ** 0.5).then_inc(exp_ready, 1)

            def body(i):
                for k in range(RING):
                    stage_ahead(act, c["other"][:, 1], idx_slot, got, staged, i, k)
                    take(i, k, 2)
                    exponentials(i, k, 1)
            for u in range(AHEAD):
                stage_ahead(act, c["other"][:, 1], idx_slot, got, staged, 0, u, 0)
            take(0, 0, 0)
            take(0, 0, 1)
            exponentials(0, 0, 0)
            each_round(act, NIT, body)
            act.wait_ge(var_ready, 1)
            act.activation(stats[:, 2, :], stats[:, 1, :], ACT.Sqrt).then_inc(std_ready, 1)

        @block.tensor
        def _(pe):
            def turn(i, k, ahead):
                u, slot = in_slots(i, k, ahead)
                pe.wait_ge(sel_ready, at(i, RING, k + ahead + 1))
                wait_for(pe, sel_turned_ready, at(i, RING, k + ahead - 1))
                for j in range(UT):
                    last = pe.transpose(ps[:, slot % 2, j * 128:(j + 1) * 128], sel[:, slot, j, :], ident[:])
                last.then_inc(sel_turned_ps, 1)

            def tops(i, k, ahead):
                u, slot = in_slots(i, k, ahead)
                pe.wait_ge(sel_turned_ready, at(i, RING, k + ahead + 1))
                wait_for(pe, shifted_ready, at(i, RING, k + ahead - 1))
                n = pe.value_load(bucket[0:1, bass.ds(u, 1)], min_val=0, max_val=NB - 1)
                for j in range(UT):
                    last = pe.matmul(ps[:, 2 + slot % 2, j * H:(j + 1) * H], sel_turned[0:NR, slot % 2, j, :],
                                     top[:, bass.ds(n, 1), :].rearrange("p o h -> p (o h)"), start=True, stop=True)
                last.then_inc(top_rows, 1)

            def body(i):
                for k in range(RING):
                    turn(i, k, 2)
                    tops(i, k, 1)
                    pe.wait_ge(weighted_ready, at(i, RING, k + 1))
                    wait_for(pe, added, at(i, RING, k + 1 - RING))
                    for j in range(UT):
                        last = pe.matmul(ps[0:NR, 4 + k, 0:D + H], sel[:, k, j, 0:NR], weighted[:, k, j, :],
                                         start=(j == 0), stop=(j == UT - 1))
                    last.then_inc(summed, 1)
            turn(0, 0, 0)
            turn(0, 0, 1)
            tops(0, 0, 0)
            each_round(pe, NIT, body)
            pe.wait_ge(w_loaded, 64)
            pe.wait_ge(added, NU)
            pe.wait_ge(sel_turned_ready, NU + 2)
            pe.wait_ge(shifted_ready, NU + 1)
            turn_and_multiply(pe, slots, ident, ps_turned, turned_slots, [wo], ps_product, dense)

        @block.vector
        def _(dve):
            step = Steps(dve, dstep)
            step(dve.memset(acc[:], 0.0))

            def select(i, k, ahead):
                u, slot = in_slots(i, k, ahead)
                wait_for(dve, summed, at(i, RING, k + ahead + 1 - RING))
                for j in range(UT):
                    last = select_nodes(dve, sel[:, slot, j, :], iota, record, u * UT + j)
                last.then_inc(sel_ready, 1)

            def shift(i, k, ahead):
                u, slot = in_slots(i, k, ahead)
                dve.wait_ge(top_rows, at(i, RING, k + ahead + 1))
                wait_for(dve, exp_ready, at(i, RING, k + ahead - 1))
                dve.tensor_tensor(shifted[:, slot % 2], score[:, bass.ds(u * UT, UT), :],
                                  ps[:, 2 + slot % 2, 0:UT * H].rearrange("p (j h) -> p j h", j=UT), ALU.subtract).then_inc(shifted_ready, 1)

            def weigh(i, k):
                dve.wait_ge(exp_ready, at(i, RING, k + 1))
                wait_for(dve, summed, at(i, RING, k + 1 - RING))
                dve.wait_ge(got[k], at(i, 16 * UT, 16 * UT))
                for j in range(UT):
                    last = dve.tensor_tensor(weighted[:, k, j, 0:D].rearrange("p (h d) -> p h d", h=H),
                                             rows[:, k, j, :].rearrange("p (h d) -> p h d", h=H),
                                             weighted[:, k, j, D:D + H].unsqueeze(2).to_broadcast([128, H, HD]), ALU.mult)
                last.then_inc(weighted_ready, 1)

            def body(i):
                for k in range(RING):
                    select(i, k, 3)
                    shift(i, k, 1)
                    weigh(i, k)
                    if k or not isinstance(i, int):
                        add_unit(dve, i, k - 1, acc, ps[0:NR, 4 + (k - 1) % RING, 0:D + H], bucket, summed, added)
            for u in range(3):
                select(0, 0, u)
            shift(0, 0, 0)
            each_round(dve, NIT, body)
            add_unit(dve, NIT, -1, acc, ps[0:NR, 4 + RING - 1, 0:D + H], bucket, summed, added)
            dve.wait_ge(added, NU)
            total = acc[:, :, D:D + H]
            step(dve.tensor_scalar(empty[:], total, 0.0, None, ALU.is_equal))
            step(dve.tensor_tensor(total, total, empty[:], ALU.add))
            step(dve.reciprocal(total, total))
            for n in range(NB):
                rest = v[:, n, :].rearrange("p (h d) -> p h d", h=H)
                sums = acc[:, n, 0:D].rearrange("p (h d) -> p h d", h=H)
                dve.tensor_tensor(rest, rest, empty[:, n, :].unsqueeze(2).to_broadcast([NR, H, HD]), ALU.mult)
                last = dve.tensor_tensor(sums, sums, total[:, n, :].unsqueeze(2).to_broadcast([NR, H, HD]), ALU.mult)
            step(last)
            step(dve.tensor_tensor(acc[:, :, 0:D], acc[:, :, 0:D], v[:], ALU.add))
            dve.wait_ge(w_loaded, 64)
            step(dve.tensor_tensor(h[:], h[:], bias[:, 0, :].unsqueeze(1).to_broadcast([NR, NB, D]), ALU.add))
            feed_products(dve, lambda n, slot: dve.tensor_copy(slot, acc[:, n, 0:D]),
                          lambda n, _, product: dve.tensor_tensor(h[:, n, :], h[:, n, :], product, ALU.add),
                          slots, ps_turned, turned_slots, ps_product, dense)
            center(step, h[:], h[:], v[:], stats, var_ready)
            dve.wait_ge(std_ready, 1)
            step(dve.reciprocal(stats[:, 2, :], stats[:, 2, :]))
            step(dve.tensor_tensor(h[:], h[:], wide(stats[:, 2, :]), ALU.mult))
            step(dve.tensor_tensor(h[:], h[:], bias[:, 1, :].unsqueeze(1).to_broadcast([NR, NB, D]), ALU.mult))
            step(dve.tensor_tensor(x[:], x[:], bias[:, 2, :].unsqueeze(1).to_broadcast([NR, NB, D]), ALU.add))
            step(dve.tensor_tensor(x[:], x[:], h[:], ALU.add))


def layer_3(nc, t, c):
    with ExitStack() as ctx:
        b = {}
        b["tab_dst"] = nc.dram_tensor("tab_dst", (N, HA), F32).ap()
        b["tab_feats"] = nc.dram_tensor("tab_feats", (N, D), F32).ap()
        b["score"] = ctx.enter_context(nc.sbuf_tensor("l3_score", [128, NT, H], F32))
        with nc.sbuf_tensor("l3_hid_src", [NR + 1, NB, HA], F32) as hid_src:
            b["hid_src"] = hid_src
            layer_3_nodes(nc, t, c, b)
            layer_3_scores(nc, t, c, b)
        layer_3_pool(nc, t, c, b)


def layer_3_nodes(nc, t, c, b):
    x, ident = c["x"], c["ident"]
    hid_src = b["hid_src"]
    with Phase(nc, "l3a") as phase:
        sb, sem = phase.sb, phase.sem

        stats = sb("stats", [NR, 3, NB])
        w1 = sb("w1", [128, H, 2, D])
        w2 = sb("w2", [128, H, 2, HD])
        b1 = sb("b1", [128, H, 2])
        b2 = sb("b2", [HD, H])
        b_rows = sb("b_rows", [3 * H, 128])
        a1 = sb("a1", [HD, H, 2, ATT])
        ab1 = sb("ab1", [NR, HA])
        slots = sb("slots", [NR, TG, D])
        turned_slots = sb("turned_slots", [128, TG, 2, NR])
        hidden = sb("hidden", [128, 2, TG, NR])
        feats = sb("feats", [HD, 2, TG, NR])
        dst_out = sb("dst_out", [NR, TG, HA])
        feats_out = sb("feats_out", [NR, TG, D])
        ps = phase.psum("ps", [128, 8, 512], F32)
        PARTS = ((0, 3), (3, 5))

        w_loaded, dstep, var_ready, std_ready = (sem(n) for n in ("w_loaded", "dstep", "var_ready", "std_ready"))
        bias_turned, bias_ready = sem("bias_turned"), sem("bias_ready")
        filled, turned, turned_taken, hidden_ps, hidden_ready, feats_ps, feats_ready, node_ps, node_taken = (
            sem(n) for n in ("filled", "turned", "turned_taken", "hidden_ps", "hidden_ready", "feats_ps", "feats_ready",
                             "node_ps", "node_taken"))
        rows_ready, rows_stored, edge_row_loaded = sem("rows_ready"), sem("rows_stored"), sem("edge_row_loaded")
        centered = sem("centered")
        block = phase.ctx.enter_context(nc.Block())
        groups = NB // TG

        @block.sync
        def _(sp):
            for hd in range(H):
                sp.dma_start(w1[:, hd], t["L3_gnn_W1"][hd].rearrange("(k p) d -> p k d", p=128)).then_inc(w_loaded, 16)
                sp.dma_start(w2[:, hd], t["L3_gnn_W2"][hd].rearrange("(k p) d -> p k d", p=128)).then_inc(w_loaded, 16)
                sp.dma_start(a1[:, hd], t["L3_gnn_A1"][hd, 0:2 * HD, :].rearrange("(k p) d -> p k d", p=HD)).then_inc(w_loaded, 16)
            sp.wait_ge(dstep, 1)
            for k in range(2):
                sp.dma_start(b_rows[k * H:(k + 1) * H, :], t["L3_gnn_b1"][:, k * 128:(k + 1) * 128]).then_inc(w_loaded, 16)
            sp.dma_start(b_rows[2 * H:3 * H, 0:HD], t["L3_gnn_b2"]).then_inc(w_loaded, 16)
            sp.dma_start(ab1[:], bcast_rows(t["L3_gnn_ab1"].rearrange("h a -> (h a)"), NR)).then_inc(w_loaded, 16)
            sp.wait_ge(centered, 1)
            for hd in range(H):
                sp.dma_start(hid_src[NR:NR + 1, :, hd * ATT:(hd + 1) * ATT],
                             t["L3_gnn_A1"][hd, 2 * HD:ATT, :].unsqueeze(1).to_broadcast([1, NB, ATT])).then_inc(edge_row_loaded, 16)
            with sp.Fori(0, groups) as g:
                sp.wait_ge(rows_ready, at(g, 1, 1))
                for tab, rows in ((b["tab_dst"], dst_out), (b["tab_feats"], feats_out)):
                    sp.dma_start(tab.rearrange("(p b) d -> p b d", b=NB)[:, bass.ds(g * TG, TG), :], rows[:]).then_inc(rows_stored, 16)
            sp.wait_ge(rows_stored, groups * 32)
            sp.wait_ge(edge_row_loaded, 16 * H)

        @block.scalar
        def _(act):
            act.wait_ge(var_ready, 1)
            act.activation(stats[:, 2, :], stats[:, 1, :], ACT.Sqrt).then_inc(std_ready, 1)
            act.wait_ge(bias_ready, 1)

            def take_feats(g, hd):
                act.wait_ge(feats_ps, at(g, H, hd + 1))
                wait_for(act, node_ps, at(g, H * TG, (hd - 1) * TG))
                for s, (lo, hi) in enumerate(PARTS):
                    last = act.activation(feats[:, hd % 2, lo:hi, :], ps[0:HD, 4 + s, 0:(hi - lo) * NR].rearrange("p (j n) -> p j n", n=NR),
                                          ACT.Identity, bias=b2[:, hd:hd + 1])
                last.then_inc(feats_ready, 1)

            def body(g):
                for hd in range(H):
                    act.wait_ge(hidden_ps, at(g, H, hd + 1))
                    wait_for(act, feats_ps, at(g, H, hd))
                    for m in range(2):
                        for s, (lo, hi) in enumerate(PARTS):
                            last = act.activation(hidden[:, m, lo:hi, :], ps[:, 2 * m + s, 0:(hi - lo) * NR].rearrange("p (j n) -> p j n", n=NR),
                                                  ACT.Relu, bias=b1[:, hd, m:m + 1])
                    last.then_inc(hidden_ready, 1)
                    take_feats(g, hd)
            each_round(act, groups, body)

        @block.tensor
        def _(pe):
            pe.wait_ge(w_loaded, 16 * 16)
            pe.transpose(ps[:, 7, 0:3 * H], b_rows[:], ident[0:3 * H, 0:3 * H]).then_inc(bias_turned, 1)
            pe.wait_ge(bias_ready, 1)

            def nodes(g, hd):
                pe.wait_ge(feats_ready, at(g, H, hd + 1))
                for j in range(TG):
                    n = hd * TG + j
                    wait_for(pe, node_taken, at(g, H * TG, n - 1))
                    bank, lhs = ps[0:NR, 6 + n % 2, :], feats[:, hd % 2, j, :]
                    for half in range(2):
                        pe.matmul(bank[:, half * ATT:(half + 1) * ATT], lhs, a1[:, hd, half, :], start=True, stop=True)
                    pe.transpose(bank[:, 2 * ATT:2 * ATT + HD], lhs, ident[0:HD, 0:HD]).then_inc(node_ps, 1)

            def body(g):
                for j in range(TG):
                    pe.wait_ge(filled, at(g, TG, j + 1))
                    if j == 0:
                        wait_for(pe, hidden_ready, at(g, H, 0))
                    if j == 4:
                        pe.wait_ge(turned_taken, at(g, TG, 1))
                    for k in range(2):
                        last = pe.transpose(ps[:, j % 4, k * NR:(k + 1) * NR], slots[:, j, k * 128:(k + 1) * 128], ident[0:NR, 0:NR])
                    last.then_inc(turned, 1)
                pe.wait_ge(turned_taken, at(g, TG, TG))
                for hd in range(H):
                    wait_for(pe, hidden_ready, at(g, H, hd))
                    for m in range(2):
                        for s, (lo, hi) in enumerate(PARTS):
                            for k in range(2):
                                last = pe.matmul(ps[:, 2 * m + s, 0:(hi - lo) * NR], w1[:, hd, k, m * 128:(m + 1) * 128],
                                                 turned_slots[:, lo:hi, k, :], start=(k == 0), stop=(k == 1))
                    last.then_inc(hidden_ps, 1)
                    if hd:
                        nodes(g, hd - 1)
                    pe.wait_ge(hidden_ready, at(g, H, hd + 1))
                    wait_for(pe, feats_ready, at(g, H, hd))
                    for s, (lo, hi) in enumerate(PARTS):
                        for m in range(2):
                            last = pe.matmul(ps[0:HD, 4 + s, 0:(hi - lo) * NR], w2[:, hd, m, :], hidden[:, m, lo:hi, :],
                                             start=(m == 0), stop=(m == 1))
                    last.then_inc(feats_ps, 1)
                nodes(g, H - 1)
            each_round(pe, groups, body)

        @block.vector
        def _(dve):
            step = Steps(dve, dstep)
            scratch = hid_src[:].rearrange("p b a -> p (b a)")[0:NR, 0:2 * NB * D].rearrange("p (k b d) -> p k b d", k=2, b=NB)
            step(dve.memset(b_rows[:], 0.0))
            center(step, x[:], scratch[:, 0], scratch[:, 1], stats, var_ready)
            dve.wait_ge(std_ready, 1)
            step(dve.reciprocal(stats[:, 2, :], stats[:, 2, :]))
            dve.sem_inc(centered, 1)
            dve.wait_ge(edge_row_loaded, 16 * H)
            dve.wait_ge(bias_turned, 1)
            step(dve.tensor_copy(b1[:], ps[:, 7, 0:2 * H].rearrange("p (k h) -> p h k", k=2)))
            dve.tensor_copy(b2[:], ps[0:HD, 7, 2 * H:3 * H]).then_inc(bias_ready, 1)

            def body(g):
                for j in range(TG):
                    wait_for(dve, turned, at(g, TG, 0))
                    n = g * TG + j
                    dve.tensor_scalar(slots[:, j, :], x[:, bass.ds(n, 1), :].rearrange("p o d -> p (o d)"), stats[:, 0, bass.ds(n, 1)],
                                      stats[:, 2, bass.ds(n, 1)], ALU.subtract, ALU.mult).then_inc(filled, 1)
                for j in range(TG):
                    dve.wait_ge(turned, at(g, TG, j + 1))
                    wait_for(dve, hidden_ps, at(g, H, 0))
                    dve.tensor_scalar(turned_slots[:, j, :, :], ps[:, j % 4, 0:2 * NR].rearrange("p (k n) -> p k n", k=2),
                                      0.0, None, ALU.max).then_inc(turned_taken, 1)
                for hd in range(H):
                    for j in range(TG):
                        n = hd * TG + j
                        dve.wait_ge(node_ps, at(g, H * TG, n + 1))
                        if n == 0:
                            wait_for(dve, rows_stored, at(g, 32, 0))
                        bank, cols = ps[0:NR, 6 + n % 2, :], slice(hd * ATT, (hd + 1) * ATT)
                        dve.tensor_copy(hid_src[0:NR, bass.ds(g * TG + j, 1), cols], bank[:, 0:ATT].unsqueeze(1))
                        dve.tensor_tensor(dst_out[:, j, cols], bank[:, ATT:2 * ATT], ab1[:, cols], ALU.add)
                        dve.tensor_copy(feats_out[:, j, hd * HD:(hd + 1) * HD], bank[:, 2 * ATT:2 * ATT + HD]).then_inc(node_taken, 1)
                dve.wait_ge(node_taken, at(g, H * TG, H * TG))
                dve.sem_inc(rows_ready, 1)
            each_round(dve, groups, body)


def layer_3_scores(nc, t, c, b):
    iota, ident = c["iota"], c["ident"]
    record, bucket = c["record"][:, 0], c["bucket"][:, 0]
    with Phase(nc, "l3b") as phase:
        sb, sem = phase.sb, phase.sem

        score, hid_src = b["score"], b["hid_src"]
        a2 = sb("a2", [128, HA])
        idx_slot = sb("idx_slot", [128, RING, UT], I32)
        rows = sb("rows", [128, RING, UT, HA])
        sel = sb("sel", [128, RING, UT, 128])
        sel_turned = sb("sel_turned", [128, 2, UT, 128])
        hid = sb("hid", [128, 2, UT, HA])
        dots = sb("dots", [128, 2, UT, H])
        ps = phase.psum("ps", [128, 6, 512], F32)

        a2_loaded, dstep, staged, apart, sel_ready, sel_turned_ps, sel_turned_ready = (
            sem(n) for n in ("a2_loaded", "dstep", "staged", "apart", "sel_ready", "sel_turned_ps", "sel_turned_ready"))
        src_ps, hid_ready, relu_ready, scored = (sem(n) for n in ("src_ps", "hid_ready", "relu_ready", "scored"))
        hid_units = sem("hid_units")
        got = [sem(f"got{k}") for k in range(RING)]
        block = phase.ctx.enter_context(nc.Block())

        @block.sync
        def _(sp):
            sp.dma_start(a2[:], bcast_rows(t["L3_gnn_A2"].rearrange("h a o -> (h a o)"), 128)).then_inc(a2_loaded, 16)

        @block.gpsimd
        def _(pool):
            gather_rows(pool, b["tab_dst"], idx_slot, lambda k, j: rows[:, k, j, :], got, staged, apart, hid_units)

        @block.scalar
        def _(act):
            def take(i, k, ahead):
                u, slot = in_slots(i, k, ahead)
                act.wait_ge(sel_turned_ps, at(i, RING, k + ahead + 1))
                wait_for(act, src_ps, at(i, RING * UT, (k + ahead - 1) * UT))
                act.copy(sel_turned[:, slot % 2], ps[:, slot % 2, 0:UT * 128].rearrange("p (j n) -> p j n", j=UT)).then_inc(sel_turned_ready, 1)

            def body(i):
                for k in range(RING):
                    stage_ahead(act, c["other"][:, 0], idx_slot, got, staged, i, k)
                    take(i, k, 1)
                    act.wait_ge(hid_units, at(i, RING, k + 1))
                    flat = hid[:, k % 2].rearrange("p j a -> p (j a)")
                    act.activation(flat, flat, ACT.Relu).then_inc(relu_ready, 1)
            for u in range(AHEAD):
                stage_ahead(act, c["other"][:, 0], idx_slot, got, staged, 0, u, 0)
            take(0, 0, 0)
            each_round(act, NIT, body)

        @block.tensor
        def _(pe):
            def turn(i, k, ahead):
                u, slot = in_slots(i, k, ahead)
                pe.wait_ge(sel_ready, at(i, RING, k + ahead + 1))
                wait_for(pe, sel_turned_ready, at(i, RING, k + ahead - 1))
                for j in range(UT):
                    last = pe.transpose(ps[:, slot % 2, j * 128:(j + 1) * 128], sel[:, slot, j, :], ident[:])
                last.then_inc(sel_turned_ps, 1)

            def body(i):
                for k in range(RING):
                    turn(i, k, 2)
                    pe.wait_ge(sel_turned_ready, at(i, RING, k + 1))
                    n = pe.value_load(bucket[0:1, bass.ds(i * RING + k, 1)], min_val=0, max_val=NB - 1)
                    for j in range(UT):
                        wait_for(pe, hid_ready, at(i, RING * UT, (k - 1) * UT + j + 1))
                        for half in range(2):
                            last = pe.matmul(ps[:, 2 + 2 * j + half, 0:HA // 2], sel_turned[0:NR + 1, k % 2, j, :],
                                             hid_src[:, bass.ds(n, 1), half * (HA // 2):(half + 1) * (HA // 2)].rearrange("p o a -> p (o a)"),
                                             start=True, stop=True)
                        last.then_inc(src_ps, 1)
            turn(0, 0, 0)
            turn(0, 0, 1)
            each_round(pe, NIT, body)

        @block.vector
        def _(dve):
            dve.memset(sel[:], 0.0)
            dve.memset(score[:], 0.0).then_inc(dstep, 1)
            dve.wait_ge(dstep, 1)
            dve.wait_ge(a2_loaded, 16)

            def select(i, k, ahead):
                u, slot = in_slots(i, k, ahead)
                wait_for(dve, sel_turned_ps, at(i, RING, k + ahead + 1 - RING))
                for j in range(UT):
                    select_nodes(dve, sel[:, slot, j, 0:NR], iota, record, u * UT + j)
                dve.tensor_copy(sel[:, slot, :, NR], record[:, bass.ds(u * UT, UT), 2]).then_inc(sel_ready, 1)

            def dot(i, k):
                slot = k % 2
                dve.wait_ge(relu_ready, at(i, RING, k + 1))
                for j in range(UT):
                    for hd in range(H):
                        cols = slice(hd * ATT, (hd + 1) * ATT)
                        last = dve.tensor_tensor_reduce(hid[:, slot, j, cols], hid[:, slot, j, cols], a2[:, cols], 1.0, 0.0,
                                                        ALU.mult, ALU.add, dots[:, slot, j, hd:hd + 1])
                last.then_inc(dstep, 1)
                dve.wait_ge(dstep, at(i, RING, k + 2))
                dve.tensor_copy(score[:, bass.ds((i * RING + k) * UT, UT), :], dots[:, slot]).then_inc(scored, 1)

            def body(i):
                for k in range(RING):
                    select(i, k, 3)
                    dve.wait_ge(got[k], at(i, 16 * UT, 16 * UT))
                    wait_for(dve, scored, at(i, RING, k - 1))
                    for j in range(UT):
                        dve.wait_ge(src_ps, at(i, RING * UT, k * UT + j + 1))
                        last = dve.tensor_tensor(hid[:, k % 2, j, :].rearrange("p (s a) -> p s a", s=2),
                                                 rows[:, k, j, :].rearrange("p (s a) -> p s a", s=2),
                                                 ps[:, 2 + 2 * j:4 + 2 * j, 0:HA // 2], ALU.add)
                        last.then_inc(hid_ready, 1)
                    dve.wait_ge(hid_ready, at(i, RING * UT, (k + 1) * UT))
                    dve.sem_inc(hid_units, 1)
                    if k or not isinstance(i, int):
                        dot(i, k - 1)
            for u in range(3):
                select(0, 0, u)
            each_round(dve, NIT, body)
            dot(NIT, -1)
            dve.wait_ge(scored, NU)


def layer_3_pool(nc, t, c, b):
    x, iota = c["x"], c["iota"]
    record, bucket = c["record"][:, 0], c["bucket"][:, 0]
    with Phase(nc, "l3c") as phase:
        sb, sem = phase.sb, phase.sem

        score = b["score"]
        acc = sb("acc", [NR, NB, D + H])
        bias = sb("bias", [128, H])
        barred = sb("barred", [128, NT])
        top = sb("top", [128, 2, H])
        idx_slot = sb("idx_slot", [128, RING, UT], I32)
        rows = sb("rows", [128, RING, UT, D])
        sel = sb("sel", [128, RING, UT, 128])
        weighted = sb("weighted", [128, RING, UT, D + H])
        ps = phase.psum("ps", [128, RING, 512], F32)

        bias_loaded, dstep, top_ready, tops_ready, shifted_ready, exp_ready = (
            sem(n) for n in ("bias_loaded", "dstep", "top_ready", "tops_ready", "shifted_ready", "exp_ready"))
        staged, apart, sel_ready, weights_ready, weighted_ready, summed, added = (
            sem(n) for n in ("staged", "apart", "sel_ready", "weights_ready", "weighted_ready", "summed", "added"))
        got = [sem(f"got{k}") for k in range(RING)]
        block = phase.ctx.enter_context(nc.Block())

        @block.sync
        def _(sp):
            sp.dma_start(bias[:], bcast_rows(t["L3_gnn_ab2"].rearrange("h o -> (h o)"), 128)).then_inc(bias_loaded, 16)

        @block.gpsimd
        def _(pool):
            pool.wait_ge(top_ready, 1)
            pool.partition_all_reduce(top[:, 1, :], top[:, 0, :], 128, bass.bass_isa.ReduceOp.max).then_inc(tops_ready, 1)
            gather_rows(pool, b["tab_feats"], idx_slot, lambda k, j: rows[:, k, j, :], got, staged, apart, weighted_ready)

        @block.scalar
        def _(act):
            for u in range(AHEAD):
                stage_ahead(act, c["other"][:, 0], idx_slot, got, staged, 0, u, 0)
            act.wait_ge(shifted_ready, 1)
            act.activation(score[:], score[:], ACT.Exp).then_inc(exp_ready, 1)
            act.wait_ge(exp_ready, 1)

            def body(i):
                for k in range(RING):
                    wait_for(act, summed, at(i, RING, k + 1 - RING))
                    act.copy(weighted[:, k, :, D:D + H], score[:, bass.ds((i * RING + k) * UT, UT), :]).then_inc(weights_ready, 1)
                    stage_ahead(act, c["other"][:, 0], idx_slot, got, staged, i, k)
            each_round(act, NIT, body)

        @block.tensor
        def _(pe):
            def body(i):
                for k in range(RING):
                    pe.wait_ge(sel_ready, at(i, RING, k + 1))
                    pe.wait_ge(weighted_ready, at(i, RING, k + 1))
                    pe.wait_ge(weights_ready, at(i, RING, k + 1))
                    wait_for(pe, added, at(i, RING, k + 1 - RING))
                    for j in range(UT):
                        last = pe.matmul(ps[0:NR, k, 0:D + H], sel[:, k, j, 0:NR], weighted[:, k, j, :],
                                         start=(j == 0), stop=(j == UT - 1))
                    last.then_inc(summed, 1)
            each_round(pe, NIT, body)

        @block.vector
        def _(dve):
            step = Steps(dve, dstep)
            dve.memset(acc[:], 0.0)
            step(dve.tensor_scalar(barred[:], record[:, :, 1], float(NR), -BIG, ALU.is_ge, ALU.mult))
            dve.wait_ge(bias_loaded, 16)
            step(dve.tensor_tensor(score[:], score[:], bias[:].unsqueeze(1).to_broadcast([128, NT, H]), ALU.add))
            step(dve.scalar_tensor_tensor(score[:], score[:], 0.2, score[:], ALU.mult, ALU.max))
            step(dve.tensor_tensor(score[:], score[:], barred[:].unsqueeze(2).to_broadcast([128, NT, H]), ALU.add))
            dve.tensor_reduce(top[:, 0, :], score[:].rearrange("p t h -> p h t"), AX.X, ALU.max).then_inc(top_ready, 1)
            dve.wait_ge(tops_ready, 1)
            dve.tensor_tensor(score[:], score[:], top[:, 1, :].unsqueeze(1).to_broadcast([128, NT, H]), ALU.subtract).then_inc(shifted_ready, 1)
            dve.wait_ge(exp_ready, 1)

            def select(i, k, ahead):
                u, slot = in_slots(i, k, ahead)
                wait_for(dve, summed, at(i, RING, k + ahead + 1 - RING))
                for j in range(UT):
                    last = select_nodes(dve, sel[:, slot, j, 0:NR], iota, record, u * UT + j)
                last.then_inc(sel_ready, 1)

            def body(i):
                for k in range(RING):
                    select(i, k, 2)
                    wait_for(dve, summed, at(i, RING, k + 1 - RING))
                    dve.wait_ge(got[k], at(i, 16 * UT, 16 * UT))
                    for j in range(UT):
                        last = dve.tensor_tensor(weighted[:, k, j, 0:D].rearrange("p (h d) -> p h d", h=H),
                                                 rows[:, k, j, :].rearrange("p (h d) -> p h d", h=H),
                                                 score[:, bass.ds((i * RING + k) * UT + j, 1), :].rearrange("p o h -> p (o h)")
                                                 .unsqueeze(2).to_broadcast([128, H, HD]), ALU.mult)
                    last.then_inc(weighted_ready, 1)
                    if k or not isinstance(i, int):
                        add_unit(dve, i, k - 1, acc, ps[0:NR, (k - 1) % RING, 0:D + H], bucket, summed, added)
            select(0, 0, 0)
            select(0, 0, 1)
            each_round(dve, NIT, body)
            add_unit(dve, NIT, -1, acc, ps[0:NR, RING - 1, 0:D + H], bucket, summed, added)
            dve.wait_ge(added, NU)
            total = acc[:, :, D:D + H]
            step(dve.tensor_scalar(total, total, 1e-10, None, ALU.add))
            step(dve.reciprocal(total, total))
            for n in range(NB):
                sums = acc[:, n, 0:D].rearrange("p (h d) -> p h d", h=H)
                last = dve.tensor_tensor(sums, sums, total[:, n, :].unsqueeze(2).to_broadcast([NR, H, HD]), ALU.mult)
            step(last)
            step(dve.tensor_tensor(x[:], x[:], acc[:, :, 0:D], ALU.add))


_INS = ["x", "src", "dst", "edge_type_64", "edge_weight", "L0_gnn_weight", "L0_gnn_attn_l", "L0_gnn_attn_r",
        "L1_gnn_W1", "L1_gnn_b1", "L1_gnn_W2", "L1_gnn_b2", "L2_gnn_query_emb", "L2_gnn_Wq", "L2_gnn_bq",
        "L2_gnn_Wk", "L2_gnn_bk", "L2_gnn_Wv", "L2_gnn_bv", "L2_gnn_rel_w", "L2_gnn_Wo", "L2_gnn_bo",
        "L2_gnn_gamma", "L2_gnn_beta", "L3_gnn_W1", "L3_gnn_b1", "L3_gnn_W2", "L3_gnn_b2", "L3_gnn_A1",
        "L3_gnn_ab1", "L3_gnn_A2", "L3_gnn_ab2"]


def kernel(**inputs):
    import numpy as np
    import concourse.bacc as bacc
    from concourse.bass_utils import run_bass_kernel_spmd as run

    nc = bacc.Bacc("TRN2", target_bir_lowering=False, num_devices=1)
    arrays, t = {}, {}
    for name in _INS:
        a = np.ascontiguousarray(inputs[name])
        arrays[f"in_{name}"] = a
        t[name] = nc.dram_tensor(f"in_{name}", a.shape, mybir.dt.from_np(a.dtype), kind="ExternalInput").ap()
    out = nc.dram_tensor("out_x", (N, D), F32, kind="ExternalOutput").ap()
    make_program(nc, t, out)
    r = run(nc, [arrays], core_ids=[0])
    return r.results[0]["out_x"]
```

```python
from contextlib import ExitStack

import concourse.bass as bass
from concourse import mybir

ALU = mybir.AluOpType
ACT = mybir.ActivationFunctionType
AX = mybir.AxisListType
F32 = mybir.dt.float32
BF16 = mybir.dt.bfloat16
I32 = mybir.dt.int32

N = 3125
D = 256
E = 53125
H = 4
HD = 64
NB = 25
NR = 125
REL = 64
ATT = 2 * HD + 1
HA = H * ATT

EC = 416
ELAST = E - 127 * EC
NKEY = NB + 1
UT = 2
NU = (E + NB * (128 * UT - 1)) // (128 * UT)
RING = 4
AHEAD = 3
NT = UT * (NU + 1 + AHEAD)
NIT = NU // RING
assert NU % RING == 0
NOBODY = 200.0
RW = 4
GROUP = 8
STEPS = EC // (2 * GROUP)
DST_L0 = (2, 5)
DST_L1 = (2, 3, 5)
DST_L2 = (2, STEPS - sum(DST_L0) - sum(DST_L1) - 2)
TG = 5
BIG = 2.0 ** 100


class Steps:

    def __init__(self, eng, sem):
        self.eng, self.sem, self.n, self.i, self.per, self.inner = eng, sem, 0, None, 0, 0

    def __call__(self, ins):
        ins.then_inc(self.sem, 1)
        if self.i is None:
            self.n += 1
            self.eng.wait_ge(self.sem, self.n)
        else:
            self.inner += 1
            self.eng.wait_ge(self.sem, self.i * self.per + (self.n + self.inner))

    def enter(self, i, per):
        self.i, self.per, self.inner = i, per, 0

    def leave(self, count):
        assert self.inner == self.per, (self.inner, self.per)
        self.i, self.n = None, self.n + count * self.per


class Phase:

    def __init__(self, nc, name):
        self.nc, self.name, self.ctx, self.sems = nc, name, ExitStack(), []

    def __enter__(self):
        self.ctx.__enter__()
        return self

    def sb(self, name, shape, dt=F32):
        return self.ctx.enter_context(self.nc.sbuf_tensor(f"{self.name}_{name}", shape, dt))

    def psum(self, name, shape, dt=F32):
        return self.ctx.enter_context(self.nc.psum_tensor(f"{self.name}_{name}", shape, dt))

    def sem(self, name):
        self.sems.append(self.nc.alloc_semaphore(f"{self.name}_{name}"))
        return self.sems[-1]

    def __exit__(self, *error):
        left = self.ctx.__exit__(*error)
        if error[0] is None and self.sems:
            self.nc.clear_and_free_semaphores(self.sems)
            self.nc.all_engine_barrier()
        return left


def at(i, k, c):
    return i * k + c


def bcast_rows(vec, rows):
    return vec.rearrange("(a d) -> a d", a=1).to_broadcast([rows, vec.shape[0]])


def wide(a):
    return a.unsqueeze(2).to_broadcast([NR, NB, D])


def center(step, x, out, moments, stats, var_ready):
    dve = step.eng
    for b in range(NB):
        last = dve.bn_stats(moments[:, b, 0:6], x[:, b, :])
    step(last)
    for b in range(NB):
        last = dve.bn_aggr(moments[:, b, 6:8], moments[:, b, 0:6])
    step(last)
    dve.tensor_scalar(stats[:, 1, :], moments[:, :, 7], 1e-5, None, ALU.add).then_inc(var_ready, 1)
    step(dve.tensor_copy(stats[:, 0, :], moments[:, :, 6]))
    if out is not None:
        step(dve.tensor_tensor(out, x, wide(stats[:, 0, :]), ALU.subtract))


def tile_slot(ps, j):
    return ps[:, j % ps.shape[1], 0:256]


def since(ps, j, count):
    banks = ps.shape[1]
    return banks if j >= banks else min(count - k + j for k in range(count) if k % banks == j)


def each_round(eng, rounds, body):
    body(0)
    with eng.Fori(1, rounds) as i:
        body(i)


def wait_for(eng, sem, value):
    if not isinstance(value, int) or value > 0:
        eng.wait_ge(sem, value)


def stage_indices(act, index, slots, got, staged):
    def body(i):
        for k in range(RING):
            wait_for(act, got[k], at(i, 16 * UT, 0))
            act.copy(slots[:, k, :], index[:, bass.ds((i * RING + k) * UT, UT)]).then_inc(staged, 1)
    each_round(act, NIT, body)


def in_slots(i, k, ahead):
    return i * RING + (k + ahead), (k + ahead) % RING


def stage_ahead(act, index, slots, got, staged, i, k, ahead=AHEAD):
    u, slot = in_slots(i, k, ahead)
    wait_for(act, got[slot], at(i, 16 * UT, (k + ahead) // RING * 16 * UT))
    act.copy(slots[:, slot, :], index[:, bass.ds(u * UT, UT)]).then_inc(staged, 1)


def gather_rows(pool, table, slots, rows, got, staged, apart, freed, per=1):
    def body(i):
        for k in range(RING):
            pool.wait_ge(staged, at(i, RING, k + 1))
            wait_for(pool, freed, at(i, RING * per, (k + 1 - RING) * per))
            pool.sem_inc(apart, 1)
            for j in range(UT):
                pool.indirect_dma_start(rows(k, j), None, table,
                                        bass.IndirectOffsetOnAxis(ap=slots[:, k, j:j + 1], axis=0)).then_inc(got[k], 16)
    each_round(pool, NIT, body)


def turned_tile(ps, j):
    return tile_slot(ps, j)[:, 0:2 * NR].rearrange("p (k n) -> p k n", k=2)


def turn_and_multiply(pe, slots, ident, ps_turned, turned_slots, weights, ps_product, sems):
    filled, turned, turned_taken, multiplied, product_taken = sems
    nw = len(weights)
    for s in (turned, turned_taken):
        pe.sem_inc(s, TG)
    for s in (multiplied, product_taken):
        pe.sem_inc(s, TG * nw)
    with pe.Fori(0, NB // TG) as g:
        for j in range(TG):
            pe.wait_ge(filled, at(g, TG, j + 1))
            pe.wait_ge(turned_taken, at(g, TG, TG + j + 1 - since(ps_turned, j, TG)))
            for k in range(2):
                last = pe.transpose(tile_slot(ps_turned, j)[:, k * NR:(k + 1) * NR],
                                    slots[:, j, k * 128:(k + 1) * 128], ident[0:NR, 0:NR])
            last.then_inc(turned, 1)
        for j in range(TG):
            pe.wait_ge(turned_taken, at(g, TG, TG + j + 1))
            for m in range(nw):
                p = j * nw + m
                pe.wait_ge(product_taken, at(g, TG * nw, TG * nw + p + 1 - since(ps_product, p, TG * nw)))
                for k in range(2):
                    last = pe.matmul(tile_slot(ps_product, p)[0:NR, :], turned_slots[:, j, k, :], weights[m][:, k, :],
                                     start=(k == 0), stop=(k == 1))
                last.then_inc(multiplied, 1)


def feed_products(dve, fill, take, slots, ps_turned, turned_slots, ps_product, sems, nw=1):
    filled, turned, turned_taken, multiplied, product_taken = sems
    with dve.Fori(0, NB // TG) as g:
        for j in range(TG):
            dve.wait_ge(turned, at(g, TG, j + 1))
            fill(g * TG + j, slots[:, j, :]).then_inc(filled, 1)
        for j in range(TG):
            dve.wait_ge(turned, at(g, TG, TG + j + 1))
            dve.wait_ge(multiplied, at(g, TG * nw, (j + 1) * nw))
            dve.tensor_copy(turned_slots[:, j, :, :], turned_tile(ps_turned, j)).then_inc(turned_taken, 1)
        for p in range(TG * nw):
            dve.wait_ge(multiplied, at(g, TG * nw, TG * nw + p + 1))
            take(g * TG + p // nw, p % nw, tile_slot(ps_product, p)[0:NR, :]).then_inc(product_taken, 1)
    dve.wait_ge(product_taken, (NB + TG) * nw)


def select_nodes(dve, out, iota, record, tile):
    return dve.tensor_scalar(out, iota[:, 0:out.shape[1]], record[:, bass.ds(tile, 1), 1], None, ALU.is_equal)


def stage_places(act, c, o, first, steps, done, sems):
    staged, _, group_done = sems

    def stage(i):
        for g in range(2):
            if done or not isinstance(i, int) or i:
                act.wait_ge(group_done[g], at(i, 16 * GROUP, done * 16 * GROUP))
            cols = bass.ds(i * (2 * GROUP) + (2 * first + g) * GROUP, GROUP)
            act.copy(c["slot_i"][:, g, :], c["place"][o][:, cols])
            act.copy(c["slot_rec"][:, g, :, :], c["sorted"][o][:, cols, :]).then_inc(staged, 1)

    if not done:
        stage(0)
    if not done and steps == 2:
        stage(1)
    else:
        with act.Fori(0 if done else 1, steps) as i:
            stage(i)


def scatter_records(pool, c, rec, steps, done, sems):
    staged, taken, group_done = sems
    with pool.Fori(0, steps) as i:
        for g in range(2):
            pool.wait_ge(staged, at(i, 2, 2 * done + g + 1))
            pool.sem_inc(taken, 1)
            for k in range(GROUP):
                pool.indirect_dma_start(rec, bass.IndirectOffsetOnAxis(ap=c["slot_i"][:, g, k:k + 1], axis=0),
                                        c["slot_rec"][:, g, k, :], None).then_inc(group_done[g], 16)


def load_buckets(nc, engine, bucket, first, count=RING):
    return nc.values_load_multi_w_load_instructions(bucket[0:1, bass.ds(first, count)], engines=(engine,),
                                                    min_val=0, max_val=NB - 1, skip_runtime_bounds_check_because=(
                                                        "a unit's bucket is a sum of NB - 1 flags"))[1]


def load_buckets_before(nc, engine, bucket, i):
    if isinstance(i, int) and i == 0:
        return (None,) + tuple(load_buckets(nc, engine, bucket, 0, RING - 1))
    return load_buckets(nc, engine, bucket, i * RING - 1)


def add_unit(dve, i, k, acc, sums, b, summed, added):
    dve.wait_ge(summed, at(i, RING, k + 1))
    wait_for(dve, added, at(i, RING, k))
    dve.tensor_tensor(acc[:, bass.ds(b, 1), :], acc[:, bass.ds(b, 1), :], sums.unsqueeze(1), ALU.add).then_inc(added, 1)


def make_program(nc, t, out):
    rec_src = nc.dram_tensor("rec_src", (128 * NT, RW), F32).ap()
    rec_dst = nc.dram_tensor("rec_dst", (128 * NT, RW), F32).ap()
    top = ExitStack()
    with top:
        c = {}
        c["x"] = top.enter_context(nc.sbuf_tensor("x_nodes", [NR, NB, D], F32))
        c["iota"] = top.enter_context(nc.sbuf_tensor("iota", [128, 256], F32))
        c["row"] = top.enter_context(nc.sbuf_tensor("row", [128, 1], F32))
        c["ident"] = top.enter_context(nc.sbuf_tensor("ident", [128, 128], F32))
        c["bucket"] = top.enter_context(nc.sbuf_tensor("bucket", [128, 2, NU + AHEAD], I32))
        c["slot_i"] = top.enter_context(nc.sbuf_tensor("slot_i", [128, 2, GROUP], I32))
        c["slot_rec"] = top.enter_context(nc.sbuf_tensor("slot_rec", [128, 2, GROUP, RW], F32))
        c["dst_place"] = top.enter_context(nc.sbuf_tensor("dst_place", [128, EC], F32))
        c["dst_sorted"] = top.enter_context(nc.sbuf_tensor("dst_sorted", [128, EC, RW], F32))
        sort_edges_and_layer_0(nc, t, c, rec_src, rec_dst)
        c["record"] = top.enter_context(nc.sbuf_tensor("edge_records", [128, 2, NT, RW], F32))
        c["other"] = top.enter_context(nc.sbuf_tensor("edge_others", [128, 2, NT], I32))
        layer_1(nc, t, c, rec_src, rec_dst)
        layer_2(nc, t, c, rec_dst)
        layer_3(nc, t, c, out)


def _(sp):
                sp.dma_start(out.rearrange("(p b) d -> p b d", b=NB), c["x"][:]).then_inc(out_stored, 16)
                sp.wait_ge(out_stored, 16)


def sort_edges_and_layer_0(nc, t, c, rec_src, rec_dst):
    with Phase(nc, "sort") as phase:
        sb, sem = phase.sb, phase.sem

        iota, row, ident, bucket = c["iota"], c["row"], c["ident"], c["bucket"]
        edges_i = sb("edges_i", [128, 3, EC], I32)
        weight = sb("weight", [128, EC])
        other = sb("other", [128, 3, EC])
        blank = sb("blank", [128, NT, RW])
        before = sb("before", [128, 128])
        ones = sb("ones", [128, 128])
        arena = sb("arena", [128, 2 * NKEY * EC])
        mask = arena[:, 0:NKEY * EC].rearrange("p (b e) -> p b e", b=NKEY)
        count = arena[:, NKEY * EC:2 * NKEY * EC].rearrange("p (b e) -> p b e", b=NKEY)
        WX = D + H
        h = arena[0:NR, 0:NB * D].rearrange("p (b d) -> p b d", b=NB)
        xt = arena[0:NR, 2 * NB * WX:3 * NB * WX].rearrange("p (b d) -> p b d", b=NB)
        picked = arena[0:NR, 0:NB * WX].rearrange("p (b d) -> p b d", b=NB)
        tab_right = nc.dram_tensor("tab_right", (N, WX), F32).ap()
        tab_left = nc.dram_tensor("tab_left", (N, H), F32).ap()
        h_slots = sb("h_slots", [NR, TG, D])
        turned_slots = sb("turned_slots", [128, TG, 2, NR])
        w0 = sb("w0", [128, 2, D])
        attn = sb("attn", [NR, 2, D])
        left = sb("left", [NR, NB, H])
        picked_left = sb("picked_left", [NR, NB, H])
        row_idx = sb("row_idx", [NR, 2, NB], I32)
        alpha = sb("alpha", [NR, 2, NB, H])
        alpha_1 = sb("alpha_1", [NR, NB])
        stats = sb("stats", [NR, 3, NB])
        junk = sb("junk", [NR, D])
        quot = sb("quot", [128, EC])
        quot_i = sb("quot_i", [128, EC], I32)
        rem = sb("rem", [128, EC])
        flag = sb("flag", [128, EC])
        c["place"] = place = (sb("src_place", [128, EC]), c["dst_place"])
        c["sorted"] = record = (sb("src_sorted", [128, EC, RW]), c["dst_sorted"])
        small = sb("small", [128, 8, NKEY])
        small_i = sb("small_i", [128, 2, NKEY], I32)
        reach = sb("reach", [128, NU + AHEAD, NB - 1])
        reached = sb("reached", [128, NU + AHEAD])
        ps = phase.psum("ps_counts", [128, 512], F32)
        ps_turned = phase.psum("ps_turned", [128, 4, 512], F32)
        ps_product = phase.psum("ps_product", [128, 3, 512], F32)

        loaded = sem("loaded")
        made = sem("made")
        blanked = sem("blanked")
        dstep = sem("dstep")
        counts_ready = sem("counts_ready")
        sums_ready = sem("sums_ready")
        prefilled = sem("prefilled")
        sorted_ = sem("sorted_")
        w0_loaded = sem("w0_loaded")
        std_ready = sem("std_ready")
        astep = sem("astep")
        filled = sem("filled")
        turned = sem("turned")
        turned_taken = sem("turned_taken")
        multiplied = sem("multiplied")
        product_taken = sem("product_taken")
        tables_ready = sem("tables_ready")
        tables_stored = sem("tables_stored")
        picked_ready = sem("picked_ready")
        logits_ready = sem("logits_ready")
        exps_ready = sem("exps_ready")
        staged = sem("staged")
        taken = sem("taken")
        group_done = [sem(f"group_done{g}") for g in range(2)]
        scatter = (staged, taken, group_done)
        block = phase.ctx.enter_context(nc.Block())

        @block.sync
        def _(sp):
            sp.dma_start(c["x"][:], t["x"].rearrange("(p b) d -> p b d", b=NB)).then_inc(loaded, 16)
            sp.wait_ge(blanked, 1)
            for k, name in enumerate(("src", "dst", "edge_type_64")):
                a = t[name]
                sp.dma_start(edges_i[0:127, k, :], a[0:127 * EC].rearrange("(p e) -> p e", e=EC)).then_inc(loaded, 16)
                sp.dma_start(edges_i[127:128, k, 0:ELAST], a[127 * EC:E].rearrange("(p e) -> p e", p=1)).then_inc(loaded, 16)
            a = t["edge_weight"]
            sp.dma_start(weight[0:127, :], a[0:127 * EC].rearrange("(p e) -> p e", e=EC)).then_inc(loaded, 16)
            sp.dma_start(weight[127:128, 0:ELAST], a[127 * EC:E].rearrange("(p e) -> p e", p=1)).then_inc(loaded, 16)
            sp.wait_ge(blanked, 2)
            for rec in (rec_src, rec_dst):
                sp.dma_start(rec.rearrange("(l t) w -> l t w", t=NT), blank[:]).then_inc(prefilled, 16)
            sp.dma_start(w0[:], t["L0_gnn_weight"].rearrange("(k p) d -> p k d", p=128)).then_inc(w0_loaded, 16)
            for k, name in enumerate(("L0_gnn_attn_l", "L0_gnn_attn_r")):
                sp.dma_start(attn[:, k, :], bcast_rows(t[name].rearrange("h d -> (h d)"), NR)).then_inc(w0_loaded, 16)
            for k, name in enumerate(("src", "dst")):
                sp.dma_start(row_idx[:, k, :], t[name][0:N].rearrange("(p b) -> p b", b=NB)).then_inc(w0_loaded, 16)
            sp.wait_ge(tables_ready, 1)
            sp.dma_start(tab_right.rearrange("(p b) d -> p b d", b=NB), xt).then_inc(tables_stored, 16)
            sp.dma_start(tab_left.rearrange("(p b) d -> p b d", b=NB), left[:]).then_inc(tables_stored, 16)

        @block.gpsimd
        def _(pool):
            pool.iota(iota[:], [[1, 256]], base=0, channel_multiplier=0,
                      allow_small_or_imprecise_dtypes=True)
            pool.iota(row[:], [[0, 1]], base=0, channel_multiplier=1,
                      allow_small_or_imprecise_dtypes=True).then_inc(made, 1)
            pool.wait_ge(prefilled, 32)
            scatter_records(pool, c, rec_src, STEPS, 0, scatter)
            pool.wait_ge(tables_stored, 32)
            pool.wait_ge(w0_loaded, 16 * 5)
            for b in range(NB):
                pool.indirect_dma_start(picked[:, b, :], None, tab_right, bass.IndirectOffsetOnAxis(
                    ap=row_idx[:, 1, b:b + 1], axis=0)).then_inc(picked_ready, 16)
                pool.indirect_dma_start(picked_left[:, b, :], None, tab_left, bass.IndirectOffsetOnAxis(
                    ap=row_idx[:, 0, b:b + 1], axis=0)).then_inc(picked_ready, 16)
            scatter_records(pool, c, rec_dst, DST_L0[0], STEPS, scatter)
            scatter_records(pool, c, rec_dst, DST_L0[1], STEPS + DST_L0[0], scatter)
            for g in range(2):
                pool.wait_ge(group_done[g], (STEPS + sum(DST_L0)) * GROUP * 16)

        @block.tensor
        def _(pe):
            for o in range(2):
                pe.wait_ge(counts_ready, o + 1)
                pe.matmul(ps[:, 0:NKEY], before[:], small[:, 2, :], start=True, stop=True)
                pe.matmul(ps[:, 32:32 + NKEY], ones[:], small[:, 2, :], start=True, stop=True).then_inc(sums_ready, 1)
            pe.wait_ge(w0_loaded, 16 * 5)
            turn_and_multiply(pe, h_slots, ident, ps_turned, turned_slots, [w0], ps_product,
                              (filled, turned, turned_taken, multiplied, product_taken))

        @block.vector
        def _(dve):
            step = Steps(dve, dstep)
            dve.memset(other[:, 2, :], 0.0)
            for k, fill in ((0, N), (1, N), (2, 0)):
                dve.memset(edges_i[:, k, :], fill)
            dve.memset(weight[:], 0.0).then_inc(blanked, 1)
            step(dve.memset(blank[:], 0.0))
            dve.memset(blank[:, :, 1], NOBODY).then_inc(blanked, 1)
            dve.memset(ones[:], 1.0)
            dve.memset(record[0][:], 0.0)
            step(dve.memset(record[1][:], 0.0))
            dve.wait_ge(made, 1)
            dve.tensor_scalar(ident[:], iota[:, 0:128], row[:, 0:1], None, ALU.is_equal)
            step(dve.tensor_scalar(before[:], iota[:, 0:128], row[:, 0:1], None, ALU.is_gt))
            dve.wait_ge(loaded, 16 * 9)
            step(dve.tensor_copy(other[:], edges_i[:]))
            for o in range(2):
                key = other[:, o, :]
                step(dve.tensor_scalar(quot_i[:], key, 1.0 / NB, None, ALU.mult))
                step(dve.tensor_copy(quot[:], quot_i[:]))
                step(dve.scalar_tensor_tensor(rem[:], quot[:], -float(NB), key, ALU.mult, ALU.add))
                step(dve.tensor_scalar(flag[:], rem[:], 0.0, None, ALU.is_lt))
                step(dve.tensor_tensor(quot[:], quot[:], flag[:], ALU.subtract))
                step(dve.scalar_tensor_tensor(rem[:], flag[:], float(NB), rem[:], ALU.mult, ALU.add))
                step(dve.tensor_scalar(flag[:], rem[:], float(NB), None, ALU.is_ge))
                step(dve.tensor_tensor(quot[:], quot[:], flag[:], ALU.add))
                step(dve.scalar_tensor_tensor(rem[:], flag[:], -float(NB), rem[:], ALU.mult, ALU.add))
                step(dve.tensor_scalar(flag[:], key, float(N), None, ALU.is_ge))
                step(dve.scalar_tensor_tensor(rem[:], flag[:], float(NB), rem[:], ALU.mult, ALU.add))
                step(dve.scalar_tensor_tensor(quot[:], flag[:], NOBODY - NR, quot[:], ALU.mult, ALU.add))
                step(dve.tensor_scalar(flag[:], other[:, 1 - o, :], float(N), None, ALU.is_lt))
                dve.tensor_tensor(record[o][:, :, 0], flag[:], other[:, 1 - o, :], ALU.mult)
                dve.tensor_copy(record[o][:, :, 1], quot[:])
                step(dve.tensor_copy(record[o][:, :, 2], weight[:] if o == 0 else other[:, 2, :]))
                step(dve.tensor_tensor(mask, rem[:].unsqueeze(1).to_broadcast([128, NKEY, EC]),
                                       iota[:, 0:NKEY].unsqueeze(2).to_broadcast([128, NKEY, EC]), ALU.is_equal))
                m = mask.rearrange("p b e -> p (b e)")
                step(dve.tensor_tensor_scan(count.rearrange("p b e -> p (b e)"), m, m, 0.0, ALU.add, ALU.max))
                earlier, here, mine, units, end, start, off, total = (small[:, k, :] for k in range(8))
                dve.memset(small[:, 0, 0:1], 0.0)
                step(dve.tensor_copy(small[:, 0, 1:NKEY], count[:, 0:NKEY - 1, EC - 1]))
                dve.tensor_tensor(mine, count[:, :, EC - 1], earlier, ALU.subtract).then_inc(counts_ready, 1)
                dve.wait_ge(sums_ready, o + 1)
                step(dve.tensor_scalar(small_i[:, 0, :], ps[:, 32:32 + NKEY], float(128 * UT - 1), None, ALU.add))
                step(dve.tensor_scalar(small_i[:, 1, :], small_i[:, 0, :], 7 + UT // 2, None, ALU.arith_shift_right))
                step(dve.tensor_copy(units, small_i[:, 1, :]))
                step(dve.tensor_tensor_scan(end, units, units, 0.0, ALU.add, ALU.max))
                step(dve.tensor_tensor(start, end, units, ALU.subtract))
                step(dve.tensor_tensor(off, ps[:, 0:NKEY], earlier, ALU.subtract))
                step(dve.scalar_tensor_tensor(off, start, float(128 * UT), off, ALU.mult, ALU.add))
                step(dve.tensor_scalar(off, off, -1.0, None, ALU.add))
                step(dve.tensor_tensor(count, count, off.unsqueeze(2).to_broadcast([128, NKEY, EC]), ALU.add))
                step(dve.tensor_tensor(count, count, mask, ALU.mult))
                step(dve.tensor_reduce(rem[:], count.rearrange("p b e -> p e b"), AX.X, ALU.add))
                step(dve.tensor_copy(quot_i[:], rem[:]))
                step(dve.tensor_scalar(quot_i[:], quot_i[:], 7, None, ALU.arith_shift_right))
                step(dve.tensor_copy(quot[:], quot_i[:]))
                step(dve.scalar_tensor_tensor(rem[:], quot[:], -128.0, rem[:], ALU.mult, ALU.add))
                step(dve.scalar_tensor_tensor(place[o][:], rem[:], float(NT), quot[:], ALU.mult, ALU.add))
                step(dve.tensor_tensor(reach[:], iota[:, 0:NU + AHEAD].unsqueeze(2).to_broadcast([128, NU + AHEAD, NB - 1]),
                                       small[:, 5, 1:NB].unsqueeze(1).to_broadcast([128, NU + AHEAD, NB - 1]), ALU.is_ge))
                step(dve.tensor_reduce(reached[:], reach[:], AX.X, ALU.add))
                step(dve.tensor_copy(bucket[:, o, :], reached[:]))
                dve.sem_inc(sorted_, 1)
            dve.wait_ge(std_ready, 1)
            step(dve.reciprocal(stats[:, 2, :], stats[:, 2, :]))
            with dve.Fori(0, NB // TG) as g:
                for j in range(TG):
                    dve.wait_ge(turned, at(g, TG, j + 1))
                    b = g * TG + j
                    dve.tensor_scalar(h_slots[:, j, :], c["x"][:, b, :], stats[:, 0, bass.ds(b, 1)],
                                      stats[:, 2, bass.ds(b, 1)], ALU.add, ALU.mult).then_inc(filled, 1)
                for j in range(TG):
                    dve.wait_ge(turned, at(g, TG, TG + j + 1))
                    dve.wait_ge(multiplied, at(g, TG, j + 1))
                    dve.tensor_scalar(turned_slots[:, j, :, :], turned_tile(ps_turned, j), 0.0, None,
                                      ALU.max).then_inc(turned_taken, 1)
                for j in range(TG):
                    dve.wait_ge(multiplied, at(g, TG, TG + j + 1))
                    dve.tensor_copy(xt[:, g * TG + j, 0:D], tile_slot(ps_product, j)[0:NR, :]).then_inc(product_taken, 1)
            dve.wait_ge(product_taken, NB + TG)
            dve.wait_ge(w0_loaded, 16 * 5)
            for k, to in ((1, xt[:, :, D:WX]), (0, left[:])):
                step(dve.tensor_tensor(h, xt[:, :, 0:D], attn[:, k, :].unsqueeze(1).to_broadcast([NR, NB, D]), ALU.mult))
                step(dve.tensor_reduce(to, h.rearrange("p b (h d) -> p b h d", h=H), AX.X, ALU.add))
            dve.sem_inc(tables_ready, 1)
            dve.wait_ge(picked_ready, 2 * NB * 16)
            logit, prob = alpha[:, 0], alpha[:, 1]
            step(dve.tensor_tensor(logit, picked[:, :, D:WX], picked_left[:], ALU.add))
            step(dve.scalar_tensor_tensor(logit, logit, 0.01, logit, ALU.mult, ALU.max))
            step(dve.tensor_reduce(alpha_1[:], logit, AX.X, ALU.max))
            per_head = alpha_1[:].unsqueeze(2).to_broadcast([NR, NB, H])
            dve.tensor_tensor(logit, logit, per_head, ALU.subtract).then_inc(logits_ready, 1)
            dve.wait_ge(exps_ready, 1)
            step(dve.tensor_reduce(alpha_1[:], prob, AX.X, ALU.add))
            step(dve.reciprocal(alpha_1[:], alpha_1[:]))
            step(dve.tensor_tensor(prob, prob, per_head, ALU.mult))
            mixed = picked[:, :, 0:D].rearrange("p b (h d) -> p b h d", h=H)
            for b in range(NB):
                last = dve.tensor_tensor(mixed[:, b], mixed[:, b], prob[:, b, :].unsqueeze(2).to_broadcast([NR, H, HD]), ALU.mult)
            step(last)
            summed = xt[:, :, 0:HD]
            step(dve.tensor_reduce(summed, picked[:, :, 0:D].rearrange("p b (h d) -> p b d h", h=H), AX.X, ALU.add))
            for k in range(H):
                xk = c["x"][:, :, k * HD:(k + 1) * HD]
                last = dve.tensor_tensor(xk, xk, summed, ALU.add)
            step(last)

        @block.scalar
        def _(act):
            act.wait_ge(loaded, 16 * 9)
            with act.Fori(0, NB) as b:
                act.activation(junk[:], c["x"][:, b, :], ACT.Copy, accum_out=stats[:, 0, bass.ds(b, 1)]).then_inc(astep, 1)
                act.wait_ge(astep, at(b, 1, 1))
            act.mul(stats[:, 0, :], stats[:, 0, :], -1.0 / D).then_inc(astep, 1)
            act.wait_ge(astep, NB + 1)
            with act.Fori(0, NB) as b:
                act.activation(junk[:], c["x"][:, b, :], ACT.Square, bias=stats[:, 0, bass.ds(b, 1)],
                               accum_out=stats[:, 1, bass.ds(b, 1)]).then_inc(astep, 1)
                act.wait_ge(astep, at(b, 1, NB + 2))
            act.activation(stats[:, 1, :], stats[:, 1, :], ACT.Copy, bias=1e-5, scale=1.0 / D).then_inc(astep, 1)
            act.wait_ge(astep, 2 * NB + 2)
            act.activation(stats[:, 2, :], stats[:, 1, :], ACT.Sqrt).then_inc(std_ready, 1)
            act.wait_ge(sorted_, 1)
            stage_places(act, c, 0, 0, STEPS, 0, scatter)
            act.wait_ge(sorted_, 2)
            stage_places(act, c, 1, 0, DST_L0[0], STEPS, scatter)
            act.wait_ge(logits_ready, 1)
            act.activation(alpha[:, 1], alpha[:, 0], ACT.Exp).then_inc(exps_ready, 1)
            stage_places(act, c, 1, DST_L0[0], DST_L0[1], STEPS + DST_L0[0], scatter)


def layer_1(nc, t, c, rec_src, rec_dst):
    tab_h = nc.dram_tensor("tab_h", (N, D), F32).ap()
    x, iota, ident = c["x"], c["iota"], c["ident"]
    with Phase(nc, "l1") as phase:
        sb, sem = phase.sb, phase.sem

        h = sb("h", [NR, NB, D])
        moments = sb("moments", [NR, NB, 8])
        acc = sb("acc", [NR, NB, D + 1])
        stats = sb("stats", [NR, 3, NB])
        bias = sb("bias", [NR, 2, D])
        w_rows = sb("w_rows", [128, 2, 2, D])
        w = sb("w", [128, 2, 2, D])
        slots = sb("slots", [NR, TG, D])
        turned_slots = sb("turned_slots", [128, TG, 2, NR])
        idx_slot = sb("idx_slot", [128, RING, UT], I32)
        rows = sb("rows", [128, RING, UT, D + 1])
        sel = sb("sel", [128, RING, UT, 128])
        ps = phase.psum("ps", [128, 8, 512], F32)
        ps_turned, ps_product, ps_sum = ps[:, 0:4], ps[:, 4:7], ps[:, 0:4]

        records_loaded, w_loaded, w_turned, w_ready = sem("records_loaded"), sem("w_loaded"), sem("w_turned"), sem("w_ready")
        dstep, var_ready, std_ready, h_ready, h_stored = (sem(n) for n in ("dstep", "var_ready", "std_ready", "h_ready", "h_stored"))
        others_ready = sem("others_ready")
        dense = [[sem(f"{n}{k}") for n in ("filled", "turned", "turned_taken", "multiplied", "product_taken")] for k in range(2)]
        staged, apart, sel_ready, summed, added = (sem(n) for n in ("staged", "apart", "sel_ready", "summed", "added"))
        got = [sem(f"got{k}") for k in range(RING)]
        scatter = (sem("places_staged"), sem("places_taken"), [sem(f"group_done{g}") for g in range(2)])
        block = phase.ctx.enter_context(nc.Block())

        @block.sync
        def _(sp):
            sp.dma_start(c["record"][:, 0], rec_src.rearrange("(l t) w -> l t w", t=NT)).then_inc(records_loaded, 16)
            for k in range(2):
                sp.dma_start(w_rows[:, k], t[f"L1_gnn_W{k + 1}"].rearrange("(c p) d -> p c d", p=128)).then_inc(w_loaded, 16)
                sp.dma_start(bias[:, k, :], bcast_rows(t[f"L1_gnn_b{k + 1}"], NR)).then_inc(w_loaded, 16)
            sp.wait_ge(h_ready, 1)
            sp.dma_start(tab_h.rearrange("(p b) d -> p b d", b=NB), h[:]).then_inc(h_stored, 16)

        @block.scalar
        def _(act):
            stage_places(act, c, 1, sum(DST_L0), DST_L1[0], 0, scatter)
            act.wait_ge(var_ready, 1)
            act.activation(stats[:, 2, :], stats[:, 1, :], ACT.Sqrt).then_inc(std_ready, 1)
            stage_places(act, c, 1, sum(DST_L0) + DST_L1[0], DST_L1[1], DST_L1[0], scatter)
            act.wait_ge(others_ready, 1)
            stage_indices(act, c["other"][:, 0], idx_slot, got, staged)
            stage_places(act, c, 1, sum(DST_L0) + sum(DST_L1[0:2]), DST_L1[2], sum(DST_L1[0:2]), scatter)

        @block.gpsimd
        def _(pool):
            scatter_records(pool, c, rec_dst, sum(DST_L1[0:2]), 0, scatter)
            pool.wait_ge(h_stored, 16)
            gather_rows(pool, tab_h, idx_slot, lambda k, j: rows[:, k, j, 0:D], got, staged, apart, summed)
            scatter_records(pool, c, rec_dst, DST_L1[2], sum(DST_L1[0:2]), scatter)
            for g in range(2):
                pool.wait_ge(scatter[2][g], sum(DST_L1) * GROUP * 16)

        @block.tensor
        def _(pe):
            pe.wait_ge(w_loaded, 64)
            for k in range(2):
                for i in range(2):
                    for o in range(2):
                        last = pe.transpose(ps[:, 2 * k + i, o * 128:(o + 1) * 128],
                                            w_rows[:, k, o, i * 128:(i + 1) * 128], ident[:])
            last.then_inc(w_turned, 1)
            pe.wait_ge(w_ready, 1)
            turn_and_multiply(pe, slots, ident, ps_turned, turned_slots, [w[:, 0]], ps_product, dense[0])
            pe.wait_ge(dense[0][2], NB + TG)

            def body(i):
                for k in range(RING):
                    pe.wait_ge(sel_ready, at(i, RING, k + 1))
                    wait_for(pe, added, at(i, RING, k + 1 - RING))
                    pe.wait_ge(got[k], at(i, 16 * UT, 16 * UT))
                    for j in range(UT):
                        last = pe.matmul(ps_sum[0:NR, k, 0:D + 1], sel[:, k, j, 0:NR], rows[:, k, j, :],
                                         start=(j == 0), stop=(j == UT - 1))
                    last.then_inc(summed, 1)
            each_round(pe, NIT, body)
            pe.wait_ge(added, NU)
            turn_and_multiply(pe, slots, ident, ps_turned, turned_slots, [w[:, 1]], ps_product, dense[1])

        @block.vector
        def _(dve):
            step = Steps(dve, dstep)

            def add_to_x(b, _, product):
                return dve.tensor_tensor(x[:, b, :], x[:, b, :], product, ALU.add)

            dve.memset(rows[:, :, :, D], 1.0)
            step(dve.memset(acc[:], 0.0))
            center(step, x[:], h[:], moments, stats, var_ready)
            dve.wait_ge(std_ready, 1)
            step(dve.reciprocal(stats[:, 2, :], stats[:, 2, :]))
            step(dve.scalar_tensor_tensor(h[:], h[:], 0.0, wide(stats[:, 2, :]), ALU.max, ALU.mult))
            dve.sem_inc(h_ready, 1)
            dve.wait_ge(records_loaded, 16)
            dve.tensor_copy(c["other"][:, 0], c["record"][:, 0, :, 0]).then_inc(others_ready, 1)
            dve.wait_ge(w_turned, 1)
            dve.tensor_copy(w[:].rearrange("p k i d -> p (k i) d"), ps[:, 0:4, 0:D]).then_inc(w_ready, 1)
            step(dve.tensor_tensor(bias[:, 0, :], bias[:, 0, :], bias[:, 1, :], ALU.add))
            step(dve.tensor_tensor(x[:], x[:], bias[:, 0, :].unsqueeze(1).to_broadcast([NR, NB, D]), ALU.add))
            feed_products(dve, lambda b, slot: dve.tensor_copy(slot, h[:, b, :]), add_to_x, slots, ps_turned, turned_slots, ps_product, dense[0])

            def body(i):
                for k in range(RING):
                    wait_for(dve, summed, at(i, RING, k + 1 - RING))
                    for j in range(UT):
                        last = select_nodes(dve, sel[:, k, j, 0:NR], iota, c["record"][:, 0], (i * RING + k) * UT + j)
                    last.then_inc(sel_ready, 1)
                buckets = load_buckets(nc, mybir.EngineType.DVE, c["bucket"][:, 0], i * RING)
                for k in range(RING):
                    add_unit(dve, i, k, acc, ps_sum[0:NR, k, 0:D + 1], buckets[k], summed, added)
            each_round(dve, NIT, body)
            dve.wait_ge(added, NU)
            total = stats[:, 0, :]
            step(dve.tensor_scalar(total, acc[:, :, D], 1.0, None, ALU.max))
            step(dve.reciprocal(total, total))
            step(dve.tensor_tensor(acc[:, :, 0:D], acc[:, :, 0:D], wide(total), ALU.mult))
            feed_products(dve, lambda b, slot: dve.tensor_copy(slot, acc[:, b, 0:D]), add_to_x, slots, ps_turned, turned_slots, ps_product, dense[1])


def layer_2(nc, t, c, rec_dst):
    with Phase(nc, "l2") as phase:
        sb = phase.sb
        b = {}
        b["h"] = sb("h", [NR, NB, D])
        b["v"] = sb("v", [NR, NB, D])
        b["score"] = sb("score", [128, NT, H])
        b["top"] = sb("top", [NR, NB, H])
        b["tab_k"] = nc.dram_tensor("tab_k", (N, D), F32).ap()
        b["tab_v"] = nc.dram_tensor("tab_v", (N, D), F32).ap()
        layer_2_scores(nc, t, c, b, rec_dst)
        layer_2_top(nc, c, b)
        layer_2_values(nc, t, c, b)


def layer_2_scores(nc, t, c, b, rec_dst):
    x, iota, ident = c["x"], c["iota"], c["ident"]
    record, bucket = c["record"][:, 1], c["bucket"][:, 1]
    with Phase(nc, "l2a") as phase:
        sb, sem = phase.sb, phase.sem

        h, v, score = b["h"], b["v"], b["score"]
        q = sb("q", [NR, NB, D])
        k_nodes = sb("k", [NR, NB, D])
        stats = sb("stats", [NR, 3, NB])
        moments = score[:].rearrange("p t h -> p (t h)")[0:NR, 0:NB * 8].rearrange("p (b k) -> p b k", b=NB)
        w = sb("w", [128, 3, 2, D])
        bias = sb("bias", [NR, 4, D])
        rel = sb("rel", [REL, HD])
        rel_wide = sb("rel_wide", [REL, H, HD])
        idx_slot = sb("idx_slot", [128, RING, UT], I32)
        rows = sb("rows", [128, RING, UT, D])
        slots = rows[:].rearrange("p k j d -> p (k j) d")[0:NR, 0:TG, :]
        sel = sb("sel", [128, RING, UT, 256])
        sel_turned = sb("sel_turned", [128, RING, UT, 256])
        keys = sb("keys", [128, RING, UT, D])
        turned_slots = keys[:].rearrange("p k j d -> p (k j d)")[:, 0:TG * 2 * NR].rearrange("p (j k n) -> p j k n", j=TG, k=2)
        ps = phase.psum("ps", [128, 8, 512], F32)
        ps_turned, ps_product = ps[:, 0:4], ps[:, 4:7]

        w_loaded, dstep, var_ready, std_ready = (sem(n) for n in ("w_loaded", "dstep", "var_ready", "std_ready"))
        nodes_ready, k_stored, others_ready = sem("nodes_ready"), sem("k_stored"), sem("others_ready")
        dense = [sem(n) for n in ("filled", "turned", "turned_taken", "multiplied", "product_taken")]
        staged, apart, sel_ready, sel_turned_ps, sel_turned_ready = (
            sem(n) for n in ("staged", "apart", "sel_ready", "sel_turned_ps", "sel_turned_ready"))
        rows_ps, keys_ready, products_ready, scored = (sem(n) for n in ("rows_ps", "keys_ready", "products_ready", "scored"))
        got = [sem(f"got{k}") for k in range(RING)]
        dst_loaded, v_stored, score_cleared, scored_1 = sem("dst_loaded"), sem("v_stored"), sem("score_cleared"), sem("scored_1")
        scatter = (sem("places_staged"), sem("places_taken"), [sem(f"group_done{g}") for g in range(2)])
        block = phase.ctx.enter_context(nc.Block())

        @block.sync
        def _(sp):
            for k, name in enumerate("qkv"):
                sp.dma_start(w[:, k], t[f"L2_gnn_W{name}"].rearrange("(k p) d -> p k d", p=128)).then_inc(w_loaded, 16)
                sp.dma_start(bias[:, k, :], bcast_rows(t[f"L2_gnn_b{name}"], NR)).then_inc(w_loaded, 16)
            sp.dma_start(bias[:, 3, :], bcast_rows(t["L2_gnn_query_emb"], NR)).then_inc(w_loaded, 16)
            sp.dma_start(rel[:], t["L2_gnn_rel_w"]).then_inc(w_loaded, 16)
            sp.wait_ge(nodes_ready, 1)
            sp.dma_start(b["tab_k"].rearrange("(p b) d -> p b d", b=NB), k_nodes[:]).then_inc(k_stored, 16)
            for g in range(2):
                sp.wait_ge(scatter[2][g], sum(DST_L2) * GROUP * 16)
            sp.dma_start(c["record"][:, 1], rec_dst.rearrange("(l t) w -> l t w", t=NT)).then_inc(dst_loaded, 16)
            sp.dma_start(b["tab_v"].rearrange("(p b) d -> p b d", b=NB), v[:]).then_inc(v_stored, 16)
            sp.wait_ge(v_stored, 16)

        @block.gpsimd
        def _(pool):
            scatter_records(pool, c, rec_dst, DST_L2[0], 0, scatter)
            scatter_records(pool, c, rec_dst, DST_L2[1], DST_L2[0], scatter)
            pool.wait_ge(k_stored, 16)
            gather_rows(pool, b["tab_k"], idx_slot, lambda k, j: rows[:, k, j, :], got, staged, apart, keys_ready)

        @block.scalar
        def _(act):
            first = sum(DST_L0) + sum(DST_L1)
            stage_places(act, c, 1, first, DST_L2[0], 0, scatter)
            act.wait_ge(var_ready, 1)
            act.activation(stats[:, 2, :], stats[:, 1, :], ACT.Sqrt).then_inc(std_ready, 1)
            stage_places(act, c, 1, first + DST_L2[0], DST_L2[1], DST_L2[0], scatter)
            act.wait_ge(others_ready, 1)
            for u in range(AHEAD):
                stage_ahead(act, c["other"][:, 1], idx_slot, got, staged, 0, u, 0)

            def take(i, k, ahead):
                u, slot = in_slots(i, k, ahead)
                act.wait_ge(sel_turned_ps, at(i, RING, k + ahead + 1))
                wait_for(act, rows_ps, at(i, RING, k + ahead + 1 - RING))
                act.copy(sel_turned[:, slot], ps[:, slot % 2].rearrange("p (j n) -> p j n", j=UT)).then_inc(sel_turned_ready, 1)

            def body(i):
                for k in range(RING):
                    stage_ahead(act, c["other"][:, 1], idx_slot, got, staged, i, k)
                    take(i, k, 2)
                    act.wait_ge(products_ready, at(i, RING, k + 1))
                    for hd in range(H):
                        products = keys[:, k, 1, hd * HD:(hd + 1) * HD]
                        last = act.activation(products, products, ACT.Copy,
                                              accum_out=score[:, bass.ds((i * RING + k) * UT + 1, 1), hd])
                    last.then_inc(scored_1, 1)
            act.wait_ge(score_cleared, 1)
            take(0, 0, 0)
            take(0, 0, 1)
            each_round(act, NIT, body)

        @block.tensor
        def _(pe):
            pe.wait_ge(w_loaded, 128)
            turn_and_multiply(pe, slots, ident, ps_turned, turned_slots, [w[:, k] for k in range(3)], ps_product, dense)
            pe.wait_ge(nodes_ready, 1)

            def turn(i, k, ahead):
                u, slot = in_slots(i, k, ahead)
                pe.wait_ge(sel_ready, at(i, RING, k + ahead + 1))
                wait_for(pe, sel_turned_ready, at(i, RING, k + ahead - 1))
                for j in range(UT):
                    for half in range(2):
                        last = pe.transpose(ps[:, slot % 2, (2 * j + half) * 128:(2 * j + half + 1) * 128],
                                            sel[:, slot, j, half * 128:(half + 1) * 128], ident[:])
                last.then_inc(sel_turned_ps, 1)

            def body(i):
                buckets = load_buckets(nc, mybir.EngineType.PE, bucket, i * RING)
                for k in range(RING):
                    pe.wait_ge(sel_turned_ready, at(i, RING, k + 1))
                    wait_for(pe, products_ready, at(i, RING, k - 1))
                    for j in range(UT):
                        pe.matmul(ps[:, 4 + k % 2, j * D:(j + 1) * D], sel_turned[0:REL, k, j, 128:256],
                                  rel_wide[:].rearrange("r h d -> r (h d)"), start=True, stop=True)
                    for j in range(UT):
                        last = pe.matmul(ps[:, 2 + k % 2, j * D:(j + 1) * D], sel_turned[0:NR, k, j, 0:128],
                                         q[:, bass.ds(buckets[k], 1), :].rearrange("p o d -> p (o d)"), start=True, stop=True)
                    last.then_inc(rows_ps, 1)
                    turn(i, k, 2)
            turn(0, 0, 0)
            turn(0, 0, 1)
            each_round(pe, NIT, body)

        @block.vector
        def _(dve):
            step = Steps(dve, dstep)
            dve.memset(sel[:], 0.0)
            center(step, x[:], h[:], moments, stats, var_ready)
            dve.wait_ge(std_ready, 1)
            step(dve.reciprocal(stats[:, 2, :], stats[:, 2, :]))
            step(dve.scalar_tensor_tensor(h[:], h[:], 0.0, wide(stats[:, 2, :]), ALU.max, ALU.mult))
            dve.wait_ge(w_loaded, 128)
            dve.tensor_scalar(rel_wide[:], rel[:].unsqueeze(1).to_broadcast([REL, H, HD]), 0.2, None, ALU.mult)
            step(dve.tensor_scalar(bias[:, 3, :], bias[:, 3, :], 0.1, None, ALU.mult))
            step(dve.memset(score[:], 0.0))
            dve.sem_inc(score_cleared, 1)
            nodes = (q, k_nodes, v)
            feed_products(dve, lambda n, slot: dve.tensor_tensor(slot, h[:, n, :], bias[:, 3, :], ALU.add),
                          lambda n, m, product: dve.tensor_tensor(nodes[m][:, n, :], product, bias[:, m, :], ALU.add),
                          slots, ps_turned, turned_slots, ps_product, dense, nw=3)
            dve.sem_inc(nodes_ready, 1)
            dve.wait_ge(dst_loaded, 16)
            dve.tensor_copy(c["other"][:, 1], c["record"][:, 1, :, 0]).then_inc(others_ready, 1)

            def select(i, k, ahead):
                u, slot = in_slots(i, k, ahead)
                wait_for(dve, sel_turned_ps, at(i, RING, k + ahead + 1 - RING))
                for j in range(UT):
                    tile = u * UT + j
                    dve.tensor_scalar(sel[:, slot, j, 0:NR], iota[:, 0:NR], record[:, bass.ds(tile, 1), 1], None, ALU.is_equal)
                    last = dve.tensor_scalar(sel[:, slot, j, 128:128 + REL], iota[:, 0:REL], record[:, bass.ds(tile, 1), 2], None, ALU.is_equal)
                last.then_inc(sel_ready, 1)

            def reduce(i, k):
                dve.wait_ge(products_ready, at(i, RING, k + 1))
                dve.tensor_reduce(score[:, bass.ds((i * RING + k) * UT, 1), :],
                                  keys[:, k % RING, 0].rearrange("p (h d) -> p h d", h=H).unsqueeze(1), AX.X, ALU.add).then_inc(scored, 1)

            def body(i):
                for k in range(RING):
                    select(i, k, 3)
                    dve.wait_ge(rows_ps, at(i, RING, k + 1))
                    dve.wait_ge(got[k], at(i, 16 * UT, 16 * UT))
                    wait_for(dve, scored, at(i, RING, k + 1 - RING))
                    wait_for(dve, scored_1, at(i, RING, k + 1 - RING))
                    dve.tensor_tensor(keys[:, k], rows[:, k], ps[:, 4 + k % 2].rearrange("p (j d) -> p j d", j=UT),
                                      ALU.add).then_inc(keys_ready, 1)
                    if k or not isinstance(i, int):
                        reduce(i, k - 1)
                    dve.wait_ge(keys_ready, at(i, RING, k + 1))
                    dve.tensor_tensor(keys[:, k], keys[:, k], ps[:, 2 + k % 2].rearrange("p (j d) -> p j d", j=UT),
                                      ALU.mult).then_inc(products_ready, 1)
            for u in range(3):
                select(0, 0, u)
            each_round(dve, NIT, body)
            reduce(NIT, -1)
            dve.wait_ge(scored, NU)
            dve.wait_ge(scored_1, NU)


def layer_2_top(nc, c, b):
    iota, row, ident, score, top = c["iota"], c["row"], c["ident"], b["score"], b["top"]
    record, bucket = c["record"][:, 1], c["bucket"][:, 1]
    parts = 3 * UT * H
    with Phase(nc, "l2b") as phase:
        sb, sem = phase.sb, phase.sem

        rest = sb("rest", [128, NT * H])
        pieces = sb("pieces", [128, NT // UT, 3, UT * H], BF16)
        ident_b = sb("ident_b", [128, 128], BF16)
        pick_1 = sb("pick_1", [parts, UT * H], BF16)
        pick = sb("pick", [parts, UT * H, 128], BF16)
        piece_slot = sb("piece_slot", [128, RING, parts], BF16)
        sel = sb("sel", [128, RING, UT, 128], BF16)
        barred = sb("barred", [128, 2, UT, 128], BF16)
        piece_rows = sb("piece_rows", [parts, 2, 128], BF16)
        unit_top = sb("unit_top", [NR, 2, H])
        negative = sb("negative", [128, 1])
        ps = phase.psum("ps", [128, 4, 512], F32)
        ps_turned = phase.psum("ps_turned", [128, 2, 1024], BF16)
        dstep, sel_ready, turned, rows_ready, laid, reduced, topped = (
            sem(n) for n in ("dstep", "sel_ready", "turned", "rows_ready", "laid", "reduced", "topped"))
        block = phase.ctx.enter_context(nc.Block())

        @block.scalar
        def _(act):
            def body(i):
                for k in range(RING):
                    act.wait_ge(turned, at(i, RING, k + 1))
                    wait_for(act, laid, at(i, RING, k - 1))
                    act.activation(barred[:, k % 2], ps_turned[:, k % 2, 0:UT * 128].rearrange("p (j n) -> p j n", j=UT),
                                   ACT.Identity, bias=negative[:, 0:1], scale=BIG)
                    act.copy(piece_rows[:, k % 2], ps_turned[0:parts, k % 2, UT * 128:(UT + 1) * 128]).then_inc(rows_ready, 1)
            each_round(act, NIT, body)

        @block.tensor
        def _(pe):
            def turn(i, k, ahead):
                u, slot = in_slots(i, k, ahead)
                pe.wait_ge(sel_ready, at(i, RING, k + ahead + 1))
                wait_for(pe, rows_ready, at(i, RING, k + ahead - 1))
                for j in range(UT):
                    pe.transpose(ps_turned[:, slot % 2, j * 128:(j + 1) * 128], sel[:, slot, j, :], ident_b[:])
                pe.transpose(ps_turned[0:parts, slot % 2, UT * 128:(UT + 1) * 128], piece_slot[:, slot, :], ident_b[:]).then_inc(turned, 1)

            def body(i):
                for k in range(RING):
                    turn(i, k, 1)
                    pe.wait_ge(rows_ready, at(i, RING, k + 1))
                    wait_for(pe, reduced, at(i, RING, k - 1))
                    for j in range(UT):
                        bank = ps[:, 2 * (k % 2) + j]
                        pe.matmul(bank, ident_b[:], barred[:, k % 2, j, :].unsqueeze(1).to_broadcast([128, H, 128]),
                                  start=True, stop=False)
                        for hd in range(H):
                            last = pe.matmul(bank[:, hd * 128:(hd + 1) * 128], pick[:, j * H + hd, :], piece_rows[:, k % 2],
                                             start=False, stop=(hd == H - 1))
                    last.then_inc(laid, 1)
            turn(0, 0, 0)
            each_round(pe, NIT, body)

        @block.vector
        def _(dve):
            step = Steps(dve, dstep)
            dve.memset(negative[:], -BIG)
            dve.memset(top[:], -BIG)
            dve.tensor_copy(ident_b[:], ident[:])
            step(dve.memset(pick_1[:], 0.0))
            for n in range(3):
                step(dve.scalar_tensor_tensor(pick_1[:], iota[0:parts, n * UT * H:(n + 1) * UT * H], row[0:parts, 0:1],
                                              pick_1[:], ALU.is_equal, ALU.add))
            step(dve.tensor_copy(pick[:], pick_1[:].unsqueeze(2).to_broadcast([parts, UT * H, 128])))
            flat = score[:].rearrange("p t h -> p (t h)").rearrange("p (u k) -> p u k", k=UT * H)
            left = rest[:].rearrange("p (u k) -> p u k", k=UT * H)
            step(dve.tensor_copy(pieces[:, :, 0, :], flat))
            step(dve.tensor_tensor(left, flat, pieces[:, :, 0, :], ALU.subtract))
            step(dve.tensor_copy(pieces[:, :, 1, :], left))
            step(dve.tensor_tensor(left, left, pieces[:, :, 1, :], ALU.subtract))
            step(dve.tensor_copy(pieces[:, :, 2, :], left))

            def select(i, k, ahead):
                u, slot = in_slots(i, k, ahead)
                wait_for(dve, turned, at(i, RING, k + ahead + 1 - RING))
                dve.tensor_copy(piece_slot[:, slot, :], pieces[:, bass.ds(u, 1)].rearrange("p o n k -> p (o n k)"))
                for j in range(UT):
                    last = select_nodes(dve, sel[:, slot, j, :], iota, record, u * UT + j)
                last.then_inc(sel_ready, 1)

            def merge(i, k, n):
                dve.wait_ge(reduced, at(i, RING, k + 1))
                wait_for(dve, topped, at(i, RING, k))
                dve.tensor_tensor(top[:, bass.ds(n, 1), :], top[:, bass.ds(n, 1), :], unit_top[:, k % 2, :].unsqueeze(1),
                                  ALU.max).then_inc(topped, 1)

            def body(i):
                buckets = load_buckets_before(nc, mybir.EngineType.DVE, bucket, i)
                for k in range(RING):
                    select(i, k, 3)
                    dve.wait_ge(laid, at(i, RING, k + 1))
                    wait_for(dve, topped, at(i, RING, k - 1))
                    dve.tensor_reduce(unit_top[:, k % 2, :], ps[0:NR, 2 * (k % 2):2 * (k % 2) + 2, :].rearrange(
                        "p j (h e) -> p h j e", h=H), AX.XY, ALU.max).then_inc(reduced, 1)
                    if k or not isinstance(i, int):
                        merge(i, k - 1, buckets[k])
            for u in range(3):
                select(0, 0, u)
            each_round(dve, NIT, body)
            last_bucket, = load_buckets(nc, mybir.EngineType.DVE, bucket, NU - 1, 1)
            merge(NIT, -1, last_bucket)
            dve.wait_ge(topped, NU)


def layer_2_values(nc, t, c, b):
    x, iota, ident = c["x"], c["iota"], c["ident"]
    record, bucket = c["record"][:, 1], c["bucket"][:, 1]
    with Phase(nc, "l2c") as phase:
        sb, sem = phase.sb, phase.sem

        h, v, score, top = b["h"], b["v"], b["score"], b["top"]
        acc = sb("acc", [NR, NB, D + H])
        stats = sb("stats", [NR, 3, NB])
        moments = sb("moments", [NR, NB, 8])
        empty = sb("empty", [NR, NB, H])
        wo = sb("wo", [128, 2, D])
        bias = sb("bias", [NR, 3, D])
        slots = sb("slots", [NR, TG, D])
        turned_slots = sb("turned_slots", [128, TG, 2, NR])
        idx_slot = sb("idx_slot", [128, RING, UT], I32)
        rows = sb("rows", [128, RING, UT, D])
        sel_b = sb("sel_b", [128, RING, UT, 128], BF16)
        sel = sb("sel", [128, RING, UT, 128])
        sel_turned = sb("sel_turned", [128, 2, UT, 128], BF16)
        ident_b = sb("ident_b", [128, 128], BF16)
        top_left = sb("top_left", [NR, NB, H])
        top_pieces = sb("top_pieces", [NR, NB, 3, H], BF16)
        edge_top = sb("edge_top", [128, 2, UT, H])
        shifted = sb("shifted", [128, 2, UT, H])
        weighted = sb("weighted", [128, RING, UT, D + H])
        ps = phase.psum("ps", [128, 6, 512], F32)
        ps_sel = phase.psum("ps_sel", [128, 2, 1024], BF16)
        ps_turned, ps_product = ps[:, 0:3], ps[:, 3:6]

        w_loaded, dstep, var_ready, std_ready = (sem(n) for n in ("w_loaded", "dstep", "var_ready", "std_ready"))
        dense = [sem(n) for n in ("filled", "turned", "turned_taken", "multiplied", "product_taken")]
        staged, apart, sel_ready, sel_turned_ps, sel_turned_ready = (
            sem(n) for n in ("staged", "apart", "sel_ready", "sel_turned_ps", "sel_turned_ready"))
        top_rows, shifted_ready, exp_ready, weighted_ready, summed, added = (
            sem(n) for n in ("top_rows", "shifted_ready", "exp_ready", "weighted_ready", "summed", "added"))
        biased, pieces_ready, widened, tops_taken = sem("biased"), sem("pieces_ready"), sem("widened"), sem("tops_taken")
        got = [sem(f"got{k}") for k in range(RING)]
        block = phase.ctx.enter_context(nc.Block())

        @block.sync
        def _(sp):
            sp.dma_start(wo[:], t["L2_gnn_Wo"].rearrange("(k p) d -> p k d", p=128)).then_inc(w_loaded, 16)
            for k, name in enumerate(("bo", "gamma", "beta")):
                sp.dma_start(bias[:, k, :], bcast_rows(t[f"L2_gnn_{name}"], NR)).then_inc(w_loaded, 16)

        @block.gpsimd
        def _(pool):
            gather_rows(pool, b["tab_v"], idx_slot, lambda k, j: rows[:, k, j, :], got, staged, apart, weighted_ready)
            pool.wait_ge(w_loaded, 64)
            for rows_of, k in ((h, 0), (x, 2)):
                pool.tensor_tensor(rows_of[:], rows_of[:], bias[:, k, :].unsqueeze(1).to_broadcast([NR, NB, D]), ALU.add).then_inc(biased, 1)

        @block.scalar
        def _(act):
            def take(i, k, ahead):
                u, slot = in_slots(i, k, ahead)
                act.wait_ge(sel_turned_ps, at(i, RING, k + ahead + 1))
                wait_for(act, top_rows, at(i, RING, k + ahead - 1))
                act.copy(sel_turned[:, slot % 2], ps_sel[:, slot % 2, 0:UT * 128].rearrange("p (j n) -> p j n", j=UT)).then_inc(sel_turned_ready, 1)

            def widen(i, k, ahead):
                u, slot = in_slots(i, k, ahead)
                act.wait_ge(sel_ready, at(i, RING, k + ahead + 1))
                wait_for(act, summed, at(i, RING, k + ahead + 1 - RING))
                act.copy(sel[:, slot], sel_b[:, slot]).then_inc(widened, 1)

            def exponentials(i, k, ahead):
                u, slot = in_slots(i, k, ahead)
                act.wait_ge(shifted_ready, at(i, RING, k + ahead + 1))
                wait_for(act, summed, at(i, RING, k + ahead + 1 - RING))
                act.activation(weighted[:, slot, :, D:D + H], shifted[:, slot % 2], ACT.Exp, scale=1.0 / HD ** 0.5).then_inc(exp_ready, 1)

            def body(i):
                for k in range(RING):
                    stage_ahead(act, c["other"][:, 1], idx_slot, got, staged, i, k)
                    exponentials(i, k, 1)
                    take(i, k, 3)
                    widen(i, k, 3)
            for u in range(AHEAD):
                stage_ahead(act, c["other"][:, 1], idx_slot, got, staged, 0, u, 0)
            for u in range(3):
                take(0, 0, u)
                widen(0, 0, u)
            exponentials(0, 0, 0)
            each_round(act, NIT, body)
            act.wait_ge(var_ready, 1)
            act.activation(stats[:, 2, :], stats[:, 1, :], ACT.Sqrt).then_inc(std_ready, 1)

        @block.tensor
        def _(pe):
            def turn(i, k, ahead):
                u, slot = in_slots(i, k, ahead)
                pe.wait_ge(sel_ready, at(i, RING, k + ahead + 1))
                wait_for(pe, sel_turned_ready, at(i, RING, k + ahead - 1))
                for j in range(UT):
                    last = pe.transpose(ps_sel[:, slot % 2, j * 128:(j + 1) * 128], sel_b[:, slot, j, :], ident_b[:])
                last.then_inc(sel_turned_ps, 1)

            def tops(i, k, ahead, n):
                u, slot = in_slots(i, k, ahead)
                pe.wait_ge(sel_turned_ready, at(i, RING, k + ahead + 1))
                wait_for(pe, tops_taken, at(i, RING, k + ahead - 1))
                for j in range(UT):
                    last = pe.matmul(ps[:, slot % 2, j * 3 * H:(j + 1) * 3 * H], sel_turned[0:NR, slot % 2, j, :],
                                     top_pieces[:, bass.ds(n, 1)].rearrange("p o n h -> p (o n h)"), start=True, stop=True)
                last.then_inc(top_rows, 1)

            def body(i):
                buckets = load_buckets(nc, mybir.EngineType.PE, bucket, i * RING + 2)
                for k in range(RING):
                    pe.wait_ge(widened, at(i, RING, k + 1))
                    pe.wait_ge(weighted_ready, at(i, RING, k + 1))
                    wait_for(pe, added, at(i, RING, k + 1 - RING))
                    for j in range(UT):
                        last = pe.matmul(ps[0:NR, 2 + k, 0:D + H], sel[:, k, j, 0:NR], weighted[:, k, j, :],
                                         start=(j == 0), stop=(j == UT - 1))
                    last.then_inc(summed, 1)
                    tops(i, k, 2, buckets[k])
                    turn(i, k, 3)
            pe.wait_ge(pieces_ready, 1)
            first_buckets = load_buckets(nc, mybir.EngineType.PE, bucket, 0, 2)
            turn(0, 0, 0)
            turn(0, 0, 1)
            tops(0, 0, 0, first_buckets[0])
            turn(0, 0, 2)
            tops(0, 0, 1, first_buckets[1])
            each_round(pe, NIT, body)
            pe.wait_ge(w_loaded, 64)
            pe.wait_ge(added, NU)
            pe.wait_ge(sel_turned_ready, NU + 3)
            pe.wait_ge(tops_taken, NU + 1)
            turn_and_multiply(pe, slots, ident, ps_turned, turned_slots, [wo], ps_product, dense)

        @block.vector
        def _(dve):
            step = Steps(dve, dstep)
            dve.tensor_copy(ident_b[:], ident[:])
            step(dve.memset(acc[:], 0.0))
            step(dve.tensor_copy(top_pieces[:, :, 0, :], top[:]))
            step(dve.tensor_tensor(top_left[:], top[:], top_pieces[:, :, 0, :], ALU.subtract))
            step(dve.tensor_copy(top_pieces[:, :, 1, :], top_left[:]))
            step(dve.tensor_tensor(top_left[:], top_left[:], top_pieces[:, :, 1, :], ALU.subtract))
            dve.tensor_copy(top_pieces[:, :, 2, :], top_left[:]).then_inc(pieces_ready, 1)

            def select(i, k, ahead):
                u, slot = in_slots(i, k, ahead)
                wait_for(dve, sel_turned_ps, at(i, RING, k + ahead + 1 - RING))
                wait_for(dve, widened, at(i, RING, k + ahead + 1 - RING))
                for j in range(UT):
                    last = select_nodes(dve, sel_b[:, slot, j, :], iota, record, u * UT + j)
                last.then_inc(sel_ready, 1)

            def take_tops(i, k, ahead):
                u, slot = in_slots(i, k, ahead)
                dve.wait_ge(top_rows, at(i, RING, k + ahead + 1))
                wait_for(dve, shifted_ready, at(i, RING, k + ahead - 1))
                dve.tensor_reduce(edge_top[:, slot % 2], ps[:, slot % 2, 0:UT * 3 * H].rearrange("p (j n h) -> p j h n", j=UT, n=3),
                                  AX.X, ALU.add).then_inc(tops_taken, 1)

            def shift(i, k, ahead):
                u, slot = in_slots(i, k, ahead)
                dve.wait_ge(tops_taken, at(i, RING, k + ahead + 1))
                wait_for(dve, exp_ready, at(i, RING, k + ahead - 1))
                dve.tensor_tensor(shifted[:, slot % 2], score[:, bass.ds(u * UT, UT), :],
                                  edge_top[:, slot % 2], ALU.subtract).then_inc(shifted_ready, 1)

            def weigh(i, k):
                dve.wait_ge(exp_ready, at(i, RING, k + 1))
                wait_for(dve, summed, at(i, RING, k + 1 - RING))
                dve.wait_ge(got[k], at(i, 16 * UT, 16 * UT))
                for j in range(UT):
                    last = dve.tensor_tensor(weighted[:, k, j, 0:D].rearrange("p (h d) -> p h d", h=H),
                                             rows[:, k, j, :].rearrange("p (h d) -> p h d", h=H),
                                             weighted[:, k, j, D:D + H].unsqueeze(2).to_broadcast([128, H, HD]), ALU.mult)
                last.then_inc(weighted_ready, 1)

            def body(i):
                buckets = load_buckets_before(nc, mybir.EngineType.DVE, bucket, i)
                for k in range(RING):
                    weigh(i, k)
                    take_tops(i, k, 1)
                    select(i, k, 3)
                    shift(i, k, 1)
                    if k or not isinstance(i, int):
                        add_unit(dve, i, k - 1, acc, ps[0:NR, 2 + (k - 1) % RING, 0:D + H], buckets[k], summed, added)
            for u in range(3):
                select(0, 0, u)
            take_tops(0, 0, 0)
            shift(0, 0, 0)
            each_round(dve, NIT, body)
            last_bucket, = load_buckets(nc, mybir.EngineType.DVE, bucket, NU - 1, 1)
            add_unit(dve, NIT, -1, acc, ps[0:NR, 2 + RING - 1, 0:D + H], last_bucket, summed, added)
            dve.wait_ge(added, NU)
            total = acc[:, :, D:D + H]
            step(dve.tensor_scalar(empty[:], total, 0.0, None, ALU.is_equal))
            step(dve.tensor_tensor(total, total, empty[:], ALU.add))
            step(dve.reciprocal(total, total))
            for n in range(NB):
                rest = v[:, n, :].rearrange("p (h d) -> p h d", h=H)
                sums = acc[:, n, 0:D].rearrange("p (h d) -> p h d", h=H)
                dve.tensor_tensor(rest, rest, empty[:, n, :].unsqueeze(2).to_broadcast([NR, H, HD]), ALU.mult)
                last = dve.tensor_tensor(sums, sums, total[:, n, :].unsqueeze(2).to_broadcast([NR, H, HD]), ALU.mult)
            step(last)
            step(dve.tensor_tensor(acc[:, :, 0:D], acc[:, :, 0:D], v[:], ALU.add))
            dve.wait_ge(w_loaded, 64)
            dve.wait_ge(biased, 1)
            feed_products(dve, lambda n, slot: dve.tensor_copy(slot, acc[:, n, 0:D]),
                          lambda n, _, product: dve.tensor_tensor(h[:, n, :], h[:, n, :], product, ALU.add),
                          slots, ps_turned, turned_slots, ps_product, dense)
            center(step, h[:], h[:], moments, stats, var_ready)
            dve.wait_ge(std_ready, 1)
            step(dve.reciprocal(stats[:, 2, :], stats[:, 2, :]))
            step(dve.tensor_tensor(h[:], h[:], wide(stats[:, 2, :]), ALU.mult))
            step(dve.tensor_tensor(h[:], h[:], bias[:, 1, :].unsqueeze(1).to_broadcast([NR, NB, D]), ALU.mult))
            dve.wait_ge(biased, 2)
            step(dve.tensor_tensor(x[:], x[:], h[:], ALU.add))


def layer_3(nc, t, c, out):
    with ExitStack() as ctx:
        b = {}
        b["tab_dst"] = nc.dram_tensor("tab_dst", (N, HA), F32).ap()
        b["tab_feats"] = nc.dram_tensor("tab_feats", (N, D), F32).ap()
        b["score"] = ctx.enter_context(nc.sbuf_tensor("l3_score", [128, NT, H], F32))
        with nc.sbuf_tensor("l3_hid_src", [NR + 1, NB, HA], F32) as hid_src:
            b["hid_src"] = hid_src
            layer_3_nodes(nc, t, c, b)
            layer_3_scores(nc, t, c, b)
        layer_3_pool(nc, t, c, b, out)


def layer_3_nodes(nc, t, c, b):
    x, ident = c["x"], c["ident"]
    hid_src = b["hid_src"]
    with Phase(nc, "l3a") as phase:
        sb, sem = phase.sb, phase.sem

        stats = sb("stats", [NR, 3, NB])
        moments = sb("moments", [NR, NB, 8])
        w1 = sb("w1", [128, H, 2, D])
        w2 = sb("w2", [128, H, 2, HD])
        b1 = sb("b1", [128, H, 2])
        b2 = sb("b2", [HD, H])
        b_rows = sb("b_rows", [3 * H, 128])
        a1 = sb("a1", [HD, H, 2, ATT])
        ab1 = sb("ab1", [NR, HA])
        slots = sb("slots", [NR, TG, D])
        turned_slots = sb("turned_slots", [128, TG, 2, NR])
        hidden = sb("hidden", [128, 2, TG, NR])
        feats = sb("feats", [HD, 2, TG, NR])
        dst_out = sb("dst_out", [NR, TG, HA])
        feats_out = sb("feats_out", [NR, TG, D])
        ps = phase.psum("ps", [128, 8, 512], F32)
        PARTS = ((0, 3), (3, 5))

        w_loaded, dstep, var_ready, std_ready = (sem(n) for n in ("w_loaded", "dstep", "var_ready", "std_ready"))
        bias_turned, bias_ready = sem("bias_turned"), sem("bias_ready")
        filled, turned, turned_taken, hidden_ps, hidden_ready, feats_ps, feats_ready, node_ps, node_taken = (
            sem(n) for n in ("filled", "turned", "turned_taken", "hidden_ps", "hidden_ready", "feats_ps", "feats_ready",
                             "node_ps", "node_taken"))
        rows_ready, rows_stored, edge_row_loaded = sem("rows_ready"), sem("rows_stored"), sem("edge_row_loaded")
        block = phase.ctx.enter_context(nc.Block())
        groups = NB // TG

        @block.sync
        def _(sp):
            for hd in range(H):
                sp.dma_start(w1[:, hd], t["L3_gnn_W1"][hd].rearrange("(k p) d -> p k d", p=128)).then_inc(w_loaded, 16)
                sp.dma_start(w2[:, hd], t["L3_gnn_W2"][hd].rearrange("(k p) d -> p k d", p=128)).then_inc(w_loaded, 16)
                sp.dma_start(a1[:, hd], t["L3_gnn_A1"][hd, 0:2 * HD, :].rearrange("(k p) d -> p k d", p=HD)).then_inc(w_loaded, 16)
            sp.wait_ge(dstep, 1)
            for k in range(2):
                sp.dma_start(b_rows[k * H:(k + 1) * H, :], t["L3_gnn_b1"][:, k * 128:(k + 1) * 128]).then_inc(w_loaded, 16)
            sp.dma_start(b_rows[2 * H:3 * H, 0:HD], t["L3_gnn_b2"]).then_inc(w_loaded, 16)
            sp.dma_start(ab1[:], bcast_rows(t["L3_gnn_ab1"].rearrange("h a -> (h a)"), NR)).then_inc(w_loaded, 16)
            for hd in range(H):
                sp.dma_start(hid_src[NR:NR + 1, :, hd * ATT:(hd + 1) * ATT],
                             t["L3_gnn_A1"][hd, 2 * HD:ATT, :].unsqueeze(1).to_broadcast([1, NB, ATT])).then_inc(edge_row_loaded, 16)
            with sp.Fori(0, groups) as g:
                sp.wait_ge(rows_ready, at(g, 1, 1))
                for tab, rows in ((b["tab_dst"], dst_out), (b["tab_feats"], feats_out)):
                    sp.dma_start(tab.rearrange("(p b) d -> p b d", b=NB)[:, bass.ds(g * TG, TG), :], rows[:]).then_inc(rows_stored, 16)
            sp.wait_ge(rows_stored, groups * 32)
            sp.wait_ge(edge_row_loaded, 16 * H)

        @block.scalar
        def _(act):
            act.wait_ge(var_ready, 1)
            act.activation(stats[:, 2, :], stats[:, 1, :], ACT.Sqrt).then_inc(std_ready, 1)
            act.wait_ge(bias_ready, 1)

            def take_feats(g, hd):
                act.wait_ge(feats_ps, at(g, H, hd + 1))
                wait_for(act, node_ps, at(g, H * TG, (hd - 1) * TG))
                for s, (lo, hi) in enumerate(PARTS):
                    last = act.activation(feats[:, hd % 2, lo:hi, :], ps[0:HD, 4 + s, 0:(hi - lo) * NR].rearrange("p (j n) -> p j n", n=NR),
                                          ACT.Identity, bias=b2[:, hd:hd + 1])
                last.then_inc(feats_ready, 1)

            def body(g):
                for hd in range(H):
                    act.wait_ge(hidden_ps, at(g, H, hd + 1))
                    wait_for(act, feats_ps, at(g, H, hd))
                    for m in range(2):
                        for s, (lo, hi) in enumerate(PARTS):
                            last = act.activation(hidden[:, m, lo:hi, :], ps[:, 2 * m + s, 0:(hi - lo) * NR].rearrange("p (j n) -> p j n", n=NR),
                                                  ACT.Relu, bias=b1[:, hd, m:m + 1])
                    last.then_inc(hidden_ready, 1)
                    take_feats(g, hd)
            each_round(act, groups, body)

        @block.tensor
        def _(pe):
            pe.wait_ge(w_loaded, 16 * 16)
            pe.transpose(ps[:, 7, 0:3 * H], b_rows[:], ident[0:3 * H, 0:3 * H]).then_inc(bias_turned, 1)
            pe.wait_ge(bias_ready, 1)

            def nodes(g, hd):
                pe.wait_ge(feats_ready, at(g, H, hd + 1))
                for j in range(TG):
                    n = hd * TG + j
                    wait_for(pe, node_taken, at(g, H * TG, n - 1))
                    bank, lhs = ps[0:NR, 6 + n % 2, :], feats[:, hd % 2, j, :]
                    for half in range(2):
                        pe.matmul(bank[:, half * ATT:(half + 1) * ATT], lhs, a1[:, hd, half, :], start=True, stop=True)
                    pe.transpose(bank[:, 2 * ATT:2 * ATT + HD], lhs, ident[0:HD, 0:HD]).then_inc(node_ps, 1)

            def body(g):
                for j in range(TG):
                    pe.wait_ge(filled, at(g, TG, j + 1))
                    if j == 0:
                        wait_for(pe, hidden_ready, at(g, H, 0))
                    if j == 4:
                        pe.wait_ge(turned_taken, at(g, TG, 1))
                    for k in range(2):
                        last = pe.transpose(ps[:, j % 4, k * NR:(k + 1) * NR], slots[:, j, k * 128:(k + 1) * 128], ident[0:NR, 0:NR])
                    last.then_inc(turned, 1)
                pe.wait_ge(turned_taken, at(g, TG, TG))
                for hd in range(H):
                    wait_for(pe, hidden_ready, at(g, H, hd))
                    for m in range(2):
                        for s, (lo, hi) in enumerate(PARTS):
                            for k in range(2):
                                last = pe.matmul(ps[:, 2 * m + s, 0:(hi - lo) * NR], w1[:, hd, k, m * 128:(m + 1) * 128],
                                                 turned_slots[:, lo:hi, k, :], start=(k == 0), stop=(k == 1))
                    last.then_inc(hidden_ps, 1)
                    if hd:
                        nodes(g, hd - 1)
                    pe.wait_ge(hidden_ready, at(g, H, hd + 1))
                    wait_for(pe, feats_ready, at(g, H, hd))
                    for s, (lo, hi) in enumerate(PARTS):
                        for m in range(2):
                            last = pe.matmul(ps[0:HD, 4 + s, 0:(hi - lo) * NR], w2[:, hd, m, :], hidden[:, m, lo:hi, :],
                                             start=(m == 0), stop=(m == 1))
                    last.then_inc(feats_ps, 1)
                nodes(g, H - 1)
            each_round(pe, groups, body)

        @block.vector
        def _(dve):
            step = Steps(dve, dstep)
            step(dve.memset(b_rows[:], 0.0))
            center(step, x[:], None, moments, stats, var_ready)
            dve.wait_ge(std_ready, 1)
            step(dve.reciprocal(stats[:, 2, :], stats[:, 2, :]))
            dve.wait_ge(edge_row_loaded, 16 * H)
            dve.wait_ge(bias_turned, 1)
            step(dve.tensor_copy(b1[:], ps[:, 7, 0:2 * H].rearrange("p (k h) -> p h k", k=2)))
            dve.tensor_copy(b2[:], ps[0:HD, 7, 2 * H:3 * H]).then_inc(bias_ready, 1)

            def body(g):
                for j in range(TG):
                    wait_for(dve, turned, at(g, TG, 0))
                    n = g * TG + j
                    dve.tensor_scalar(slots[:, j, :], x[:, bass.ds(n, 1), :].rearrange("p o d -> p (o d)"), stats[:, 0, bass.ds(n, 1)],
                                      stats[:, 2, bass.ds(n, 1)], ALU.subtract, ALU.mult).then_inc(filled, 1)
                for j in range(TG):
                    dve.wait_ge(turned, at(g, TG, j + 1))
                    wait_for(dve, hidden_ps, at(g, H, 0))
                    dve.tensor_scalar(turned_slots[:, j, :, :], ps[:, j % 4, 0:2 * NR].rearrange("p (k n) -> p k n", k=2),
                                      0.0, None, ALU.max).then_inc(turned_taken, 1)
                for hd in range(H):
                    for j in range(TG):
                        n = hd * TG + j
                        dve.wait_ge(node_ps, at(g, H * TG, n + 1))
                        if n == 0:
                            wait_for(dve, rows_stored, at(g, 32, 0))
                        bank, cols = ps[0:NR, 6 + n % 2, :], slice(hd * ATT, (hd + 1) * ATT)
                        dve.tensor_copy(hid_src[0:NR, bass.ds(g * TG + j, 1), cols], bank[:, 0:ATT].unsqueeze(1))
                        dve.tensor_tensor(dst_out[:, j, cols], bank[:, ATT:2 * ATT], ab1[:, cols], ALU.add)
                        dve.tensor_copy(feats_out[:, j, hd * HD:(hd + 1) * HD], bank[:, 2 * ATT:2 * ATT + HD]).then_inc(node_taken, 1)
                dve.wait_ge(node_taken, at(g, H * TG, H * TG))
                dve.sem_inc(rows_ready, 1)
            each_round(dve, groups, body)


def layer_3_scores(nc, t, c, b):
    iota, ident = c["iota"], c["ident"]
    record, bucket = c["record"][:, 0], c["bucket"][:, 0]
    with Phase(nc, "l3b") as phase:
        sb, sem = phase.sb, phase.sem

        score, hid_src = b["score"], b["hid_src"]
        a2 = sb("a2", [128, HA])
        idx_slot = sb("idx_slot", [128, RING, UT], I32)
        rows = sb("rows", [128, RING, UT, HA])
        sel = sb("sel", [128, RING, UT, 128])
        sel_turned = sb("sel_turned", [128, RING, UT, 128])
        hid = sb("hid", [128, RING, UT, HA])
        ps = phase.psum("ps", [128, 6, 512], F32)

        a2_loaded, dstep, staged, apart, sel_ready, sel_turned_ps, sel_turned_ready = (
            sem(n) for n in ("a2_loaded", "dstep", "staged", "apart", "sel_ready", "sel_turned_ps", "sel_turned_ready"))
        src_ps, hid_ready, weighted, scored = (sem(n) for n in ("src_ps", "hid_ready", "weighted", "scored"))
        got = [sem(f"got{k}") for k in range(RING)]
        block = phase.ctx.enter_context(nc.Block())

        @block.sync
        def _(sp):
            sp.dma_start(a2[:], bcast_rows(t["L3_gnn_A2"].rearrange("h a o -> (h a o)"), 128)).then_inc(a2_loaded, 16)

        @block.gpsimd
        def _(pool):
            gather_rows(pool, b["tab_dst"], idx_slot, lambda k, j: rows[:, k, j, :], got, staged, apart, hid_ready, per=UT)

        @block.scalar
        def _(act):
            def take(i, k, ahead):
                u, slot = in_slots(i, k, ahead)
                act.wait_ge(sel_turned_ps, at(i, RING, k + ahead + 1))
                wait_for(act, src_ps, at(i, RING * UT, (k + ahead + 1 - RING) * UT))
                act.copy(sel_turned[:, slot], ps[:, slot % 2, 0:UT * 128].rearrange("p (j n) -> p j n", j=UT)).then_inc(sel_turned_ready, 1)

            def body(i):
                for k in range(RING):
                    stage_ahead(act, c["other"][:, 0], idx_slot, got, staged, i, k)
                    take(i, k, 2)
                    for j in range(UT):
                        act.wait_ge(weighted, at(i, RING * UT, k * UT + j + 1))
                        for hd in range(H):
                            units = hid[:, k, j, hd * ATT:(hd + 1) * ATT]
                            last = act.activation(units, units, ACT.Copy,
                                                  accum_out=score[:, bass.ds((i * RING + k) * UT + j, 1), hd])
                    last.then_inc(scored, 1)
            act.wait_ge(dstep, 1)
            for u in range(AHEAD):
                stage_ahead(act, c["other"][:, 0], idx_slot, got, staged, 0, u, 0)
            take(0, 0, 0)
            take(0, 0, 1)
            each_round(act, NIT, body)

        @block.tensor
        def _(pe):
            def turn(i, k, ahead):
                u, slot = in_slots(i, k, ahead)
                pe.wait_ge(sel_ready, at(i, RING, k + ahead + 1))
                wait_for(pe, sel_turned_ready, at(i, RING, k + ahead - 1))
                for j in range(UT):
                    last = pe.transpose(ps[:, slot % 2, j * 128:(j + 1) * 128], sel[:, slot, j, :], ident[:])
                last.then_inc(sel_turned_ps, 1)

            def body(i):
                buckets = load_buckets(nc, mybir.EngineType.PE, bucket, i * RING)
                for k in range(RING):
                    pe.wait_ge(sel_turned_ready, at(i, RING, k + 1))
                    for j in range(UT):
                        wait_for(pe, hid_ready, at(i, RING * UT, (k - 1) * UT + j + 1))
                        for half in range(2):
                            last = pe.matmul(ps[:, 2 + 2 * j + half, 0:HA // 2], sel_turned[0:NR + 1, k, j, :],
                                             hid_src[:, bass.ds(buckets[k], 1), half * (HA // 2):(half + 1) * (HA // 2)].rearrange("p o a -> p (o a)"),
                                             start=True, stop=True)
                        last.then_inc(src_ps, 1)
                    turn(i, k, 2)
            turn(0, 0, 0)
            turn(0, 0, 1)
            each_round(pe, NIT, body)

        @block.vector
        def _(dve):
            dve.memset(sel[:], 0.0)
            dve.memset(score[:], 0.0).then_inc(dstep, 1)
            dve.wait_ge(dstep, 1)
            dve.wait_ge(a2_loaded, 16)

            def select(i, k, ahead):
                u, slot = in_slots(i, k, ahead)
                wait_for(dve, sel_turned_ps, at(i, RING, k + ahead + 1 - RING))
                for j in range(UT):
                    select_nodes(dve, sel[:, slot, j, 0:NR], iota, record, u * UT + j)
                dve.tensor_copy(sel[:, slot, :, NR], record[:, bass.ds(u * UT, UT), 2]).then_inc(sel_ready, 1)

            def body(i):
                for k in range(RING):
                    select(i, k, 3)
                    dve.wait_ge(got[k], at(i, 16 * UT, 16 * UT))
                    wait_for(dve, scored, at(i, RING, k + 1 - RING))
                    for j in range(UT):
                        dve.wait_ge(src_ps, at(i, RING * UT, k * UT + j + 1))
                        last = dve.tensor_tensor(hid[:, k, j, :].rearrange("p (s a) -> p s a", s=2),
                                                 rows[:, k, j, :].rearrange("p (s a) -> p s a", s=2),
                                                 ps[:, 2 + 2 * j:4 + 2 * j, 0:HA // 2], ALU.add)
                        last.then_inc(hid_ready, 1)
                    for j in range(UT):
                        dve.wait_ge(hid_ready, at(i, RING * UT, k * UT + j + 1))
                        dve.scalar_tensor_tensor(hid[:, k, j, :], hid[:, k, j, :], 0.0, a2[:], ALU.max, ALU.mult).then_inc(weighted, 1)
            for u in range(3):
                select(0, 0, u)
            each_round(dve, NIT, body)
            dve.wait_ge(scored, NU)


def layer_3_pool(nc, t, c, b, out):
    x, iota = c["x"], c["iota"]
    record, bucket = c["record"][:, 0], c["bucket"][:, 0]
    with Phase(nc, "l3c") as phase:
        sb, sem = phase.sb, phase.sem

        score = b["score"]
        acc = sb("acc", [NR, NB, D + H])
        bias = sb("bias", [128, H])
        barred = sb("barred", [128, NT])
        top = sb("top", [128, 2, H])
        idx_slot = sb("idx_slot", [128, RING, UT], I32)
        rows = sb("rows", [128, RING, UT, D])
        sel = sb("sel", [128, RING, UT, 128])
        weighted = sb("weighted", [128, RING, UT, D + H])
        ps = phase.psum("ps", [128, RING, 512], F32)

        bias_loaded, dstep, top_ready, tops_ready, shifted_ready, exp_ready = (
            sem(n) for n in ("bias_loaded", "dstep", "top_ready", "tops_ready", "shifted_ready", "exp_ready"))
        staged, apart, sel_ready, weights_ready, weighted_ready, summed, added = (
            sem(n) for n in ("staged", "apart", "sel_ready", "weights_ready", "weighted_ready", "summed", "added"))
        x_ready, out_stored = sem("x_ready"), sem("out_stored")
        got = [sem(f"got{k}") for k in range(RING)]
        block = phase.ctx.enter_context(nc.Block())

        @block.sync
        def _(sp):
            sp.dma_start(bias[:], bcast_rows(t["L3_gnn_ab2"].rearrange("h o -> (h o)"), 128)).then_inc(bias_loaded, 16)
            for g in range(NB // TG):
                sp.wait_ge(x_ready, g + 1)
                nodes = slice(g * TG, (g + 1) * TG)
                sp.dma_start(out.rearrange("(p b) d -> p b d", b=NB)[:, nodes, :], x[:, nodes, :]).then_inc(out_stored, 16)
            sp.wait_ge(out_stored, 16 * (NB // TG))

        @block.gpsimd
        def _(pool):
            pool.wait_ge(top_ready, 1)
            pool.partition_all_reduce(top[:, 1, :], top[:, 0, :], 128, bass.bass_isa.ReduceOp.max).then_inc(tops_ready, 1)
            gather_rows(pool, b["tab_feats"], idx_slot, lambda k, j: rows[:, k, j, :], got, staged, apart, weighted_ready)

        @block.scalar
        def _(act):
            for u in range(AHEAD):
                stage_ahead(act, c["other"][:, 0], idx_slot, got, staged, 0, u, 0)
            act.wait_ge(shifted_ready, 1)
            act.activation(score[:], score[:], ACT.Exp).then_inc(exp_ready, 1)
            act.wait_ge(exp_ready, 1)

            def body(i):
                for k in range(RING):
                    wait_for(act, summed, at(i, RING, k + 1 - RING))
                    act.copy(weighted[:, k, :, D:D + H], score[:, bass.ds((i * RING + k) * UT, UT), :]).then_inc(weights_ready, 1)
                    stage_ahead(act, c["other"][:, 0], idx_slot, got, staged, i, k)
            each_round(act, NIT, body)

        @block.tensor
        def _(pe):
            def body(i):
                for k in range(RING):
                    pe.wait_ge(sel_ready, at(i, RING, k + 1))
                    pe.wait_ge(weighted_ready, at(i, RING, k + 1))
                    pe.wait_ge(weights_ready, at(i, RING, k + 1))
                    wait_for(pe, added, at(i, RING, k + 1 - RING))
                    for j in range(UT):
                        last = pe.matmul(ps[0:NR, k, 0:D + H], sel[:, k, j, 0:NR], weighted[:, k, j, :],
                                         start=(j == 0), stop=(j == UT - 1))
                    last.then_inc(summed, 1)
            each_round(pe, NIT, body)

        @block.vector
        def _(dve):
            step = Steps(dve, dstep)
            dve.memset(acc[:], 0.0)
            step(dve.tensor_scalar(barred[:], record[:, :, 1], float(NR), -BIG, ALU.is_ge, ALU.mult))
            dve.wait_ge(bias_loaded, 16)
            step(dve.tensor_tensor(score[:], score[:], bias[:].unsqueeze(1).to_broadcast([128, NT, H]), ALU.add))
            step(dve.scalar_tensor_tensor(score[:], score[:], 0.2, score[:], ALU.mult, ALU.max))
            step(dve.tensor_tensor(score[:], score[:], barred[:].unsqueeze(2).to_broadcast([128, NT, H]), ALU.add))
            dve.tensor_reduce(top[:, 0, :], score[:].rearrange("p t h -> p h t"), AX.X, ALU.max).then_inc(top_ready, 1)
            dve.wait_ge(tops_ready, 1)
            dve.tensor_tensor(score[:], score[:], top[:, 1, :].unsqueeze(1).to_broadcast([128, NT, H]), ALU.subtract).then_inc(shifted_ready, 1)
            dve.wait_ge(exp_ready, 1)

            def select(i, k, ahead):
                u, slot = in_slots(i, k, ahead)
                wait_for(dve, summed, at(i, RING, k + ahead + 1 - RING))
                for j in range(UT):
                    last = select_nodes(dve, sel[:, slot, j, 0:NR], iota, record, u * UT + j)
                last.then_inc(sel_ready, 1)

            def body(i):
                buckets = load_buckets_before(nc, mybir.EngineType.DVE, bucket, i)
                for k in range(RING):
                    select(i, k, 2)
                    wait_for(dve, summed, at(i, RING, k + 1 - RING))
                    dve.wait_ge(got[k], at(i, 16 * UT, 16 * UT))
                    for j in range(UT):
                        last = dve.tensor_tensor(weighted[:, k, j, 0:D].rearrange("p (h d) -> p h d", h=H),
                                                 rows[:, k, j, :].rearrange("p (h d) -> p h d", h=H),
                                                 score[:, bass.ds((i * RING + k) * UT + j, 1), :].rearrange("p o h -> p (o h)")
                                                 .unsqueeze(2).to_broadcast([128, H, HD]), ALU.mult)
                    last.then_inc(weighted_ready, 1)
                    if k or not isinstance(i, int):
                        add_unit(dve, i, k - 1, acc, ps[0:NR, (k - 1) % RING, 0:D + H], buckets[k], summed, added)
            select(0, 0, 0)
            select(0, 0, 1)
            each_round(dve, NIT, body)
            last_bucket, = load_buckets(nc, mybir.EngineType.DVE, bucket, NU - 1, 1)
            add_unit(dve, NIT, -1, acc, ps[0:NR, RING - 1, 0:D + H], last_bucket, summed, added)
            dve.wait_ge(added, NU)
            total = acc[:, :, D:D + H]
            step(dve.tensor_scalar(total, total, 1e-10, None, ALU.add))
            step(dve.reciprocal(total, total))
            for g in range(NB // TG):
                nodes = slice(g * TG, (g + 1) * TG)
                for n in range(g * TG, (g + 1) * TG):
                    sums = acc[:, n, 0:D].rearrange("p (h d) -> p h d", h=H)
                    last = dve.tensor_tensor(sums, sums, total[:, n, :].unsqueeze(2).to_broadcast([NR, H, HD]), ALU.mult)
                step(last)
                dve.tensor_tensor(x[:, nodes, :], x[:, nodes, :], acc[:, nodes, 0:D], ALU.add).then_inc(x_ready, 1)


_INS = ["x", "src", "dst", "edge_type_64", "edge_weight", "L0_gnn_weight", "L0_gnn_attn_l", "L0_gnn_attn_r",
        "L1_gnn_W1", "L1_gnn_b1", "L1_gnn_W2", "L1_gnn_b2", "L2_gnn_query_emb", "L2_gnn_Wq", "L2_gnn_bq",
        "L2_gnn_Wk", "L2_gnn_bk", "L2_gnn_Wv", "L2_gnn_bv", "L2_gnn_rel_w", "L2_gnn_Wo", "L2_gnn_bo",
        "L2_gnn_gamma", "L2_gnn_beta", "L3_gnn_W1", "L3_gnn_b1", "L3_gnn_W2", "L3_gnn_b2", "L3_gnn_A1",
        "L3_gnn_ab1", "L3_gnn_A2", "L3_gnn_ab2"]


def kernel(**inputs):
    import numpy as np
    import concourse.bacc as bacc
    from concourse.bass_utils import run_bass_kernel_spmd as run

    nc = bacc.Bacc("TRN2", target_bir_lowering=False, num_devices=1)
    arrays, t = {}, {}
    for name in _INS:
        a = np.ascontiguousarray(inputs[name])
        arrays[f"in_{name}"] = a
        t[name] = nc.dram_tensor(f"in_{name}", a.shape, mybir.dt.from_np(a.dtype), kind="ExternalInput").ap()
    out = nc.dram_tensor("out_x", (N, D), F32, kind="ExternalOutput").ap()
    make_program(nc, t, out)
    r = run(nc, [arrays], core_ids=[0])
    return r.results[0]["out_x"]
```
